# Optimizing a Trainium2 kernel written in Bass

```python
import numpy as np
import jax
import jax.numpy as jnp

def _softmax(x, axis=-1):
    return jax.nn.softmax(x, axis=axis)

def _gelu(x):
    return jax.nn.gelu(x, approximate=True)

def _silu(x):
    return jax.nn.silu(x)

def _sigmoid(x):
    return jax.nn.sigmoid(x)

def _layernorm(x, axis=-1, eps=1e-05):
    m = jnp.mean(x, axis=axis, keepdims=True)
    v = jnp.var(x, axis=axis, keepdims=True)
    return (x - m) / jnp.sqrt(v + eps)

def _scatter_add(tgt, idx, src, axis=0):
    return tgt.at[idx].add(src)

def _segment_sum(src, seg, n):
    return jax.ops.segment_sum(src, seg, n)
kernel_name = 'mk_cond_resid_d1_seqx_r4_689616'

def setup_inputs(seed: int=0):
    np.random.seed(seed)
    _w = jnp.asarray

    def _rec_inputs():
        import jax
        import jax.numpy as jnp
        _rk = jax.random.key(seed)
        x = -5.13e-06 + 0.01765 * jax.random.normal(jax.random.fold_in(_rk, 1), (2, 1024, 256), jnp.float32)
        _lenS = 1024 - jax.random.randint(jax.random.fold_in(_rk, 7), (2,), 0, max(1, 1024 // 4) + 1, jnp.int32)
        _lenS2 = 1024 - jax.random.randint(jax.random.fold_in(_rk, 8), (2,), 0, max(1, 1024 // 4) + 1, jnp.int32)
        cond_1024 = 0.0061147 + 1.02565 * jax.random.normal(jax.random.fold_in(_rk, 11), (2, 256), jnp.float32)
        return (x, cond_1024)
    x, cond_1024 = _rec_inputs()

    def _L0_cond_setup():
        import math
        import jax, jax.numpy as jnp
        import numpy as np
        EPS = 1e-07
        MAX_TANH_ARG = 1.0 - 1e-05

        def _norm(x):
            return jnp.sqrt(jnp.sum(x * x, axis=-1, keepdims=True)).clip(EPS)

        def logmap0(x):
            n = _norm(x)
            return jnp.arctanh(jnp.clip(n, EPS, MAX_TANH_ARG)) * x / n

        def expmap0(v):
            n = _norm(v)
            return jnp.tanh(n) * v / n

        def mobius_add(x, y):
            x2 = jnp.sum(x * x, -1, keepdims=True)
            y2 = jnp.sum(y * y, -1, keepdims=True)
            xy = jnp.sum(x * y, -1, keepdims=True)
            num = (1 + 2 * xy + y2) * x + (1 - x2) * y
            den = (1 + 2 * xy + x2 * y2).clip(EPS)
            return num / den

        def plin(x, w, b):
            return expmap0(logmap0(x) @ w + b)

        def layer_norm(x, eps=1e-06):
            m = x.mean(-1, keepdims=True)
            v = ((x - m) ** 2).mean(-1, keepdims=True)
            return (x - m) / jnp.sqrt(v + eps)

        def _beta(a, b):
            return math.exp(math.lgamma(a) + math.lgamma(b) - math.lgamma(a + b))
        D, H, FF = (256, 16, 1024)
        HD = D // H
        BETA_N = _beta(D / 2, 0.5)
        BETA_H = _beta(HD / 2, 0.5)

        def _to_heads(p):
            B, S, _ = p.shape
            t = logmap0(p).reshape(B, S, H, HD) * (BETA_H / BETA_N)
            return expmap0(jnp.transpose(t, (0, 2, 1, 3)))

        def _from_heads(ph):
            B, _, S, _ = ph.shape
            t = logmap0(ph) * (BETA_N / BETA_H)
            t = jnp.transpose(t, (0, 2, 1, 3)).reshape(B, S, D)
            return expmap0(t)
        key = jax.random.key(seed)
        ks = jax.random.split(key, 20)
        B, S = (4, 256)
        x = expmap0(0.02 * jax.random.normal(ks[0], (B, S, D), jnp.float32))
        t_emb = jax.random.normal(ks[1], (B, 1, D), jnp.float32)
        g = lambda k, sh: 0.02 * jax.random.normal(k, sh, jnp.float32)
        return {'x': x, 't_emb': t_emb, 'w_q': g(ks[2], (D, D)), 'b_q': jnp.zeros((D,), jnp.float32), 'w_k': g(ks[3], (D, D)), 'b_k': jnp.zeros((D,), jnp.float32), 'w_v': g(ks[4], (D, D)), 'b_v': jnp.zeros((D,), jnp.float32), 'w_o': g(ks[5], (D, D)), 'b_o': jnp.zeros((D,), jnp.float32), 'w_f1': g(ks[6], (D, FF)), 'b_f1': jnp.zeros((FF,), jnp.float32), 'w_f2': g(ks[7], (FF, D)), 'b_f2': jnp.zeros((D,), jnp.float32), 'w_ada': g(ks[8], (D, 6 * D)), 'b_ada': jnp.zeros((6 * D,), jnp.float32)}
    _L0_cond_all = _L0_cond_setup()
    _L0_cond_in = {k: v for k, v in _L0_cond_all.items() if k in ('w_q', 'b_q', 'w_k', 'b_k', 'w_v', 'b_v', 'w_o', 'b_o', 'w_f1', 'b_f1', 'w_f2', 'b_f2', 'w_ada', 'b_ada')}
    del _L0_cond_all
    return {'x': x, 'cond_1024': cond_1024, 'L0_cond_w_q': _L0_cond_in['w_q'], 'L0_cond_b_q': _L0_cond_in['b_q'], 'L0_cond_w_k': _L0_cond_in['w_k'], 'L0_cond_b_k': _L0_cond_in['b_k'], 'L0_cond_w_v': _L0_cond_in['w_v'], 'L0_cond_b_v': _L0_cond_in['b_v'], 'L0_cond_w_o': _L0_cond_in['w_o'], 'L0_cond_b_o': _L0_cond_in['b_o'], 'L0_cond_w_f1': _L0_cond_in['w_f1'], 'L0_cond_b_f1': _L0_cond_in['b_f1'], 'L0_cond_w_f2': _L0_cond_in['w_f2'], 'L0_cond_b_f2': _L0_cond_in['b_f2'], 'L0_cond_w_ada': _L0_cond_in['w_ada'], 'L0_cond_b_ada': _L0_cond_in['b_ada']}

def reference(x, cond_1024, L0_cond_w_q, L0_cond_b_q, L0_cond_w_k, L0_cond_b_k, L0_cond_w_v, L0_cond_b_v, L0_cond_w_o, L0_cond_b_o, L0_cond_w_f1, L0_cond_b_f1, L0_cond_w_f2, L0_cond_b_f2, L0_cond_w_ada, L0_cond_b_ada):
    import jax
    import jax.numpy as jnp

    def _L0_cond_ref(x, t_emb, w_q, b_q, w_k, b_k, w_v, b_v, w_o, b_o, w_f1, b_f1, w_f2, b_f2, w_ada, b_ada):
        import math
        import jax, jax.numpy as jnp
        import numpy as np
        EPS = 1e-07
        MAX_TANH_ARG = 1.0 - 1e-05

        def _norm(x):
            return jnp.sqrt(jnp.sum(x * x, axis=-1, keepdims=True)).clip(EPS)

        def logmap0(x):
            n = _norm(x)
            return jnp.arctanh(jnp.clip(n, EPS, MAX_TANH_ARG)) * x / n

        def expmap0(v):
            n = _norm(v)
            return jnp.tanh(n) * v / n

        def mobius_add(x, y):
            x2 = jnp.sum(x * x, -1, keepdims=True)
            y2 = jnp.sum(y * y, -1, keepdims=True)
            xy = jnp.sum(x * y, -1, keepdims=True)
            num = (1 + 2 * xy + y2) * x + (1 - x2) * y
            den = (1 + 2 * xy + x2 * y2).clip(EPS)
            return num / den

        def plin(x, w, b):
            return expmap0(logmap0(x) @ w + b)

        def layer_norm(x, eps=1e-06):
            m = x.mean(-1, keepdims=True)
            v = ((x - m) ** 2).mean(-1, keepdims=True)
            return (x - m) / jnp.sqrt(v + eps)

        def _beta(a, b):
            return math.exp(math.lgamma(a) + math.lgamma(b) - math.lgamma(a + b))
        D, H, FF = (256, 16, 1024)
        HD = D // H
        BETA_N = _beta(D / 2, 0.5)
        BETA_H = _beta(HD / 2, 0.5)

        def _to_heads(p):
            B, S, _ = p.shape
            t = logmap0(p).reshape(B, S, H, HD) * (BETA_H / BETA_N)
            return expmap0(jnp.transpose(t, (0, 2, 1, 3)))

        def _from_heads(ph):
            B, _, S, _ = ph.shape
            t = logmap0(ph) * (BETA_N / BETA_H)
            t = jnp.transpose(t, (0, 2, 1, 3)).reshape(B, S, D)
            return expmap0(t)
        ada = t_emb @ w_ada + b_ada
        sh_msa, sc_msa, g_msa, sh_mlp, sc_mlp, g_mlp = jnp.split(ada, 6, axis=-1)
        residual = x
        xn = layer_norm(logmap0(x))
        xm = expmap0(xn * (1 + sc_msa) + sh_msa)
        q = _to_heads(plin(xm, w_q, b_q))
        k = _to_heads(plin(xm, w_k, b_k))
        v = _to_heads(plin(xm, w_v, b_v))
        qt, kt, vt = (logmap0(q), logmap0(k), logmap0(v))
        scores = jnp.einsum('bhqd,bhkd->bhqk', qt, kt) / math.sqrt(HD)
        attn = jax.nn.softmax(scores, axis=-1)
        out_h = expmap0(jnp.einsum('bhqk,bhkd->bhqd', attn, vt))
        attn_out = plin(_from_heads(out_h), w_o, b_o)
        attn_t = g_msa * logmap0(attn_out)
        x = mobius_add(residual, expmap0(attn_t))
        residual = x
        xn = layer_norm(logmap0(x))
        xm = expmap0(xn * (1 + sc_mlp) + sh_mlp)
        ff = plin(plin(xm, w_f1, b_f1), w_f2, b_f2)
        ff_t = g_mlp * logmap0(ff)
        return mobius_add(residual, expmap0(ff_t))
    x = x + _L0_cond_ref(x, cond_1024[:, None, :], L0_cond_w_q, L0_cond_b_q, L0_cond_w_k, L0_cond_b_k, L0_cond_w_v, L0_cond_b_v, L0_cond_w_o, L0_cond_b_o, L0_cond_w_f1, L0_cond_b_f1, L0_cond_w_f2, L0_cond_b_f2, L0_cond_w_ada, L0_cond_b_ada)
    return x

_drawn_inputs = setup_inputs


def setup_inputs(seed=0):
    import zlib

    import numpy as np

    out = dict(_drawn_inputs(seed))
    spreads = {'L0_cond_b_q': (0.0, 0.8),
     'L0_cond_b_k': (0.0, 0.8),
     'L0_cond_b_v': (0.0, 0.1),
     'L0_cond_b_o': (0.0, 0.1),
     'L0_cond_b_f1': (0.0, 0.1),
     'L0_cond_b_f2': (0.0, 0.1),
     'L0_cond_b_ada': (0.0, 0.1)}
    factors = {'L0_cond_w_q': 8.0, 'L0_cond_w_k': 8.0}
    for name, (base, spread) in spreads.items():
        noise = np.random.default_rng([zlib.crc32(name.encode()), seed]).standard_normal(out[name].shape)
        drawn = base * np.exp(spread * noise) if base else spread * noise
        out[name] = jnp.asarray(drawn.astype(out[name].dtype))
    for name, factor in factors.items():
        out[name] = (out[name] * factor).astype(out[name].dtype)
    return out
```

```python
import math
from contextlib import ExitStack

import numpy as np

import concourse.bass as bass
from concourse import mybir

F32 = mybir.dt.float32
F16 = mybir.dt.float16
I32 = mybir.dt.int32
ALU = mybir.AluOpType
ACT = mybir.ActivationFunctionType
AX_X = mybir.AxisListType.X

P = 128
B, S, D, H, FF = 2, 1024, 256, 16, 1024
HD = D // H
KD = D // P
KF = FF // P
TILES = B * S // P
TB = TILES // B
CH = 2
HG = 4
QW = 512
GROUPS = B * (S // QW) * (H // HG)
STEPS = 4
UNIT_TILES = QW // P

EPS = 1e-7
EPS2 = EPS * EPS
MAX_TANH = float(np.float32(1.0 - 1e-5))
A = math.atanh(MAX_TANH)


def _beta(a, b):
    return math.exp(math.lgamma(a) + math.lgamma(b) - math.lgamma(a + b))


C = _beta(HD / 2, 0.5) / _beta(D / 2, 0.5)
assert C * C > H and A * A / math.sqrt(HD) < 60

SH1, SC1, G1, SH2, SC2, G2 = range(6)


def group(g):
    n = H // HG
    return g // (2 * n), g // n % 2, g % n


def timeline():
    fill = {}

    def put(step, *jobs):
        fill.setdefault(step, []).extend(jobs)

    out = [("ada", 0)]
    for c in range(TB // CH):
        out += [("u", c), ("uT", c), ("za", c), ("zb", c), ("split", c), ("qkT", CH * c), ("qkT", CH * c + 1)]
        if c == 0:
            out.append(("fold", 0))
    out.append(("stage", 0))
    for c, s in zip(range(TB // CH, TILES // CH), (0, 6, 13, 20)):
        put(s, ("u", c))
        put(s + 1, ("uT", c))
        put(s + 2, ("za", c))
        put(s + 3, ("zb", c), ("split", c))
        put(s + 6, ("qkT", CH * c))
        put(s + 7, ("qkT", CH * c + 1))

    def unit(v, s):
        put(s, ("oT", 2 * v), ("oT", 2 * v + 1))
        put(s + 1, ("y", 2 * v), ("y", 2 * v + 1), ("mid", v))
        put(s + 4, ("mid_tanh", v))
        put(s + 6, ("u2T", 2 * v), ("u2T", 2 * v + 1), ("ff", 4 * v), ("ff", 4 * v + 1))
        put(s + 7, ("ff", 4 * v + 2), ("ff", 4 * v + 3), ("end", v))
        put(s + 9, ("end_tanh", v))

    for v, s in enumerate((30, 41, 52)):
        unit(v, s)
    last = GROUPS * STEPS
    for s in range(last):
        out.append(("att", s))
        g = s // STEPS
        if s % STEPS == 0:
            if g:
                out.append(("acc", g - 1))
            if g + 1 < GROUPS:
                out.append(("stage", g + 1))
        if s % STEPS == 1 and g:
            out.append(("accT", g - 1))
        out += fill.pop(s, [])
    out += [("att_end", last), ("acc", GROUPS - 1), ("accT", GROUPS - 1)]
    unit(3, last)
    for s in sorted(fill):
        out += fill[s]
    return out


TIMELINE = timeline()


def uses_of_banks():
    at, count = {}, [0, 0]

    def use(bank, *key):
        at[key] = (bank, count[bank])
        count[bank] += 1

    for kind, n in TIMELINE:
        if kind in ("uT", "zb", "accT"):
            use(0, kind, n)
        elif kind in ("za", "qkT"):
            use(0, kind, n)
            use(1, kind + "1", n)
        elif kind in ("oT", "y", "u2T", "ff"):
            use(n % 2, kind, n)
    return at


BANK_USE = uses_of_banks()


def build(nc, x, cond_t, w_ada, b_ada, w_qkv, b_qkv, w_o, b_o, w_f1, b_f1, w_f2, b_f2, out):
    with ExitStack() as ctx:
        def sb(name, shape, dt=F32):
            return ctx.enter_context(nc.sbuf_tensor(name, shape, dt))

        def sem(name):
            return ctx.enter_context(nc.semaphore(name))

        x_sb = sb("x_sb", [P, TILES, D])
        qT = sb("qT", [P, B, H // 2, S], F16)
        kT = sb("kT", [P, B, H // 2, S], F16)
        kz = sb("kz", [P, 2, HG, S], F16)
        v1 = sb("v1", [P, TILES, H, HD + 1])
        probs = sb("probs", [P, 2, 2, HG, QW])
        attn0 = sb("attn0", [P, TB, D])
        accT = sb("accT", [P, QW])
        wo_sb = sb("wo_sb", [P, KD, D])
        fg = sb("fg", [P, KD, 2 * D])
        fg_row = sb("fg_row", [P, 2 * D])
        wqkv_sb = sb("wqkv_sb", [P, KD, 3 * D])
        bqkv_sb = sb("bqkv_sb", [P, 3 * D])
        bo_sb = sb("bo_sb", [P, D])
        b2_sb = sb("b2_sb", [P, D])
        mods = sb("mods", [P, B, 6, D])
        identf = sb("identf", [P, P])
        ident = sb("ident", [P, P], F16)
        scratch = sb("scratch", [P, 4608])
        small = sb("small", [P, 780])

        u = scratch[:, 0:512].rearrange("p (t d) -> p t d", t=CH)
        uT = scratch[:, 512:1024].rearrange("p (t k m) -> p t k m", t=CH, k=KD)
        z = scratch[:, 1024:2560].rearrange("p (t n) -> p t n", t=CH)
        sq = scratch[:, 2560:4096]
        q_parts = scratch[:, 2560:3584].bitcast(F16).rearrange("p (h s e) -> p h s e", s=4, e=HD)
        k_parts = scratch[:, 3584:4608].bitcast(F16).rearrange("p (h s e) -> p h s e", s=4, e=HD)
        ut4 = UNIT_TILES * D
        y_sb = scratch[:, 0:ut4].rearrange("p (t d) -> p t d", d=D)
        x1 = scratch[:, ut4:2 * ut4].rearrange("p (t d) -> p t d", d=D)
        u2 = scratch[:, 2 * ut4:3 * ut4].rearrange("p (t d) -> p t d", d=D)
        tT = scratch[:, 3 * ut4:4 * ut4].rearrange("p (t k m) -> p t k m", t=UNIT_TILES, k=KD)
        dump = scratch[:, 4 * ut4:4 * ut4 + D]
        pr = probs[:].rearrange("p a b c q -> p (a b c q)")
        ada_sb = pr[:, 0:3072].rearrange("p (k n) -> p k n", k=KD)
        w2w1 = pr[:, 3072:7168].rearrange("p (f n) -> p f n", f=KF)
        b1_sb = pr[:, 7168:8192]
        w1_sb = attn0[:].rearrange("p t d -> p (t d)").rearrange("p (k n) -> p k n", k=KD)
        at_start = kz[:, 1].rearrange("p h s -> p (h s)").bitcast(F32)
        bada_sb = at_start[:, 0:1536]
        condB = at_start[:, 1536:2048].rearrange("p (k b m) -> p k b m", k=KD, b=B)
        b1cB = accT[:, 0:0 + 512]
        cond_sb = small[:, 700:704].rearrange("p (k b) -> p k b", k=KD)
        b1c_sb = small[:, 704:712]
        attn1 = kT[:, 0].rearrange("p h s -> p (h s)").bitcast(F32)[:, 0:TB * D].rearrange("p (t d) -> p t d", d=D)
        attn = [attn0[:], attn1]

        stats = small[:, 0:32].rearrange("p (t s) -> p t s", s=2)
        x_n2 = small[:, 32:48]
        x_rstd = small[:, 48:64]
        b1_n2 = small[:, 64:65]
        free = 66
        bn = small[:, 660:684]
        tanh_in, tanh_out = small[:, 684:688], small[:, 688:692]

        sc_ps = ctx.enter_context(nc.psum_tensor("sc_ps", [P, 2, 2, QW], F32))
        acc_ps = ctx.enter_context(nc.psum_tensor("acc_ps", [P, 2, QW], F32))
        wk_ps = ctx.enter_context(nc.psum_tensor("wk_ps", [P, 2, 512], F32))

        ld_x = [sem(f"ld_x{i}") for i in range(4)]
        ld_cond, ld_ada, ld_bada = sem("ld_cond"), sem("ld_ada"), sem("ld_bada")
        ld_qkv, ld_bqkv, ld_o, ld_bo = sem("ld_qkv"), sem("ld_bqkv"), sem("ld_o"), sem("ld_bo")
        ld_f1, ld_f2, ld_b1, ld_b1c, ld_b2 = sem("ld_f1"), sem("ld_f2"), sem("ld_b1"), sem("ld_b1c"), sem("ld_b2")
        idents = sem("idents")
        cond_ready = sem("cond_ready")
        ada_done = sem("ada_done")
        ada_free = sem("ada_free")
        w1T_done, w1T_ready = sem("w1T_done"), sem("w1T_ready")
        b1B_ready, b1B_used = sem("b1B_ready"), sem("b1B_used")
        fold_done, fold_ready = sem("fold_done"), sem("fold_ready")
        bank_full = [sem("bank0_full"), sem("bank1_full")]
        bank_free = [sem("bank0_free"), sem("bank1_free")]
        u_ready = sem("u_ready")
        parts_ready = sem("parts_ready")
        kz_ready = sem("kz_ready")
        scores_ready = sem("scores_ready")
        probs_ready = sem("probs_ready")
        sums_done = sem("sums_done")
        acc_ready = sem("acc_ready")
        u2_ready = sem("u2_ready")
        norm_ready, tanh_ready = sem("norm_ready"), sem("tanh_ready")
        out_ready, stored = sem("out_ready"), sem("stored")
        dve_chain, pool_chain = sem("dve_chain"), sem("pool_chain")

        block = ctx.enter_context(nc.Block())

        @block.sync
        def _(sp):
            sp.dma_start(cond_sb, cond_t).then_inc(ld_cond, 16)
            for i in range(2):
                sp.dma_start(x_sb[:, 4 * i:4 * i + 4], x[:, 4 * i:4 * i + 4]).then_inc(ld_x[i], 16)
            sp.dma_start(ada_sb, w_ada).then_inc(ld_ada, 16)
            sp.dma_start(wqkv_sb[:], w_qkv).then_inc(ld_qkv, 16)
            sp.dma_start(w1_sb, w_f1).then_inc(ld_f1, 16)
            sp.dma_start(w2w1[:, :, 0:D], w_f2).then_inc(ld_f2, 16)
            sp.dma_start(wo_sb[:], w_o).then_inc(ld_o, 16)
            for i in range(2, 4):
                sp.dma_start(x_sb[:, 4 * i:4 * i + 4], x[:, 4 * i:4 * i + 4]).then_inc(ld_x[i], 16)
            for v in range(4):
                sp.wait_ge(out_ready, v + 1)
                sp.dma_start(out[:, UNIT_TILES * v:UNIT_TILES * (v + 1)], u2).then_inc(stored, 16)
            sp.wait_ge(stored, 4 * 16)

        @block.gpsimd
        def _(pool):
            n = 0
            for t in (identf, ident):
                pool.memset(t[:], 0.0).then_inc(pool_chain, 1)
                n += 1
                pool.wait_ge(pool_chain, n)
                pool.affine_select(out=t[:], in_=t[:], compare_op=ALU.not_equal, fill=1.0, base=0,
                                   pattern=[[-1, P]], channel_multiplier=1).then_inc(idents, 1)
            pool.memset(v1[:, :, :, HD:HD + 1], 1.0).then_inc(idents, 1)
            pool.memset(kz[:, 0].bitcast(F32), 0.0).then_inc(idents, 1)

        @block.scalar
        def _(act):
            act.dma_start(bada_sb, b_ada.partition_broadcast(P)).then_inc(ld_bada, 16)
            act.dma_start(bqkv_sb[:], b_qkv.partition_broadcast(P)).then_inc(ld_bqkv, 16)
            act.dma_start(b1c_sb, b_f1[1]).then_inc(ld_b1c, 16)
            act.dma_start(b1_sb, b_f1[0].partition_broadcast(P)).then_inc(ld_b1, 16)
            act.dma_start(bo_sb[:], b_o.partition_broadcast(P)).then_inc(ld_bo, 16)
            act.dma_start(b2_sb[:], b_f2.partition_broadcast(P)).then_inc(ld_b2, 16)
            tanhs = 0
            for kind, n in TIMELINE:
                if kind == "att":
                    for i in range(4):
                        unit = 4 * n + i
                        act.wait_ge(scores_ready, unit + 1)
                        if n >= 2 and i == 0:
                            act.wait_ge(sums_done, n - 1)
                        act.activation(probs[:, n % 2, i // 2, 2 * (i % 2):2 * (i % 2) + 2], sc_ps[:, unit % 2],
                                       ACT.Exp, scale=1.0 / math.sqrt(HD)).then_inc(probs_ready, 1)
                elif kind in ("mid_tanh", "end_tanh"):
                    tanhs += 1
                    act.wait_ge(norm_ready, tanhs)
                    act.activation(tanh_out, tanh_in, ACT.Tanh).then_inc(tanh_ready, 1)


        @block.tensor
        def _(pe):
            def take(*key):
                bank, n = BANK_USE[key]
                if n:
                    pe.wait_ge(bank_free[bank], n)
                return wk_ps[:, bank], bank_full[bank]

            def sums(s):
                g = s // STEPS
                b, _, hg = group(g)
                pe.wait_ge(probs_ready, 4 * s + 4)
                if s % STEPS == 0 and g >= 2:
                    pe.wait_ge(acc_ready, g - 1)
                for k in range(2):
                    kt = 2 * (s % STEPS) + k
                    for j in range(HG):
                        mm = pe.matmul(acc_ps[32 * j:32 * j + HD + 1, g % 2], v1[:, TB * b + kt, HG * hg + j],
                                       probs[:, s % 2, k, j], start=(kt == 0), stop=(kt == TB - 1),
                                       tile_position=(0, 32 * j))
                mm.then_inc(sums_done, 1)

            for kind, n in TIMELINE:
                if kind == "ada":
                    pe.wait_ge(cond_ready, 1)
                    pe.wait_ge(ld_ada, 16)
                    for b in range(B):
                        for i in range(3):
                            bank = (sc_ps[:, 0, 0], sc_ps[:, 0, 1], sc_ps[:, 1, 0],
                                    sc_ps[:, 1, 1], acc_ps[:, 0], acc_ps[:, 1])[3 * b + i]
                            for k in range(KD):
                                mm = pe.matmul(bank, condB[:, k, b], ada_sb[:, k, 512 * i:512 * (i + 1)],
                                               start=(k == 0), stop=(k == KD - 1))
                            mm.then_inc(ada_done, 1)
                elif kind == "fold":
                    pe.wait_ge(ld_f1, 16)
                    pe.wait_ge(ada_free, 6)
                    for f in range(KF):
                        for k in range(KD):
                            mm = pe.transpose(sc_ps[:, f // 4, f // 2 % 2, 256 * (f % 2) + P * k:256 * (f % 2) + P * (k + 1)],
                                              w1_sb[:, k, P * f:P * (f + 1)], identf[:])
                        if f % 2:
                            mm.then_inc(w1T_done, 1)
                    pe.wait_ge(ld_f2, 16)
                    pe.wait_ge(w1T_ready, 4)
                    for m in range(KD):
                        for f in range(KF):
                            mm = pe.matmul(acc_ps[:, m], w2w1[:, f, D + P * m:D + P * (m + 1)], w2w1[:, f],
                                           start=(f == 0), stop=(f == KF - 1))
                        mm.then_inc(fold_done, 1)
                    for f in range(KF):
                        if f % 4 == 0:
                            pe.wait_ge(b1B_ready, f // 4 + 1)
                        mm = pe.matmul(sc_ps[:, 0, 0], b1cB[:, P * (f % 4):P * (f % 4 + 1)], w2w1[:, f],
                                       start=(f == 0), stop=(f == KF - 1))
                        if f % 4 == 3:
                            mm.then_inc(b1B_used, 1)
                elif kind == "uT":
                    bank, full = take(kind, n)
                    pe.wait_ge(u_ready, n + 1)
                    if n == 0:
                        pe.wait_ge(idents, 4)
                    for t in range(CH):
                        for k in range(KD):
                            i = KD * t + k
                            mm = pe.transpose(bank[:, P * i:P * (i + 1)], u[:, t, P * k:P * (k + 1)], identf[:])
                    mm.then_inc(full, 1)
                elif kind in ("za", "zb"):
                    t = int(kind == "zb")
                    if n == 0:
                        pe.wait_ge(ld_qkv, 16)
                    bank, full = take(kind, n)
                    for k in range(KD):
                        mm = pe.matmul(bank, uT[:, t, k], wqkv_sb[:, k, 0:2 * D], start=(k == 0), stop=(k == KD - 1))
                    mm.then_inc(full, 1)
                    if kind == "za":
                        bank, full = take("za1", n)
                        for t in range(CH):
                            for k in range(KD):
                                mm = pe.matmul(bank[:, D * t:D * (t + 1)], uT[:, t, k], wqkv_sb[:, k, 2 * D:3 * D],
                                               start=(k == 0), stop=(k == KD - 1))
                        mm.then_inc(full, 1)
                elif kind == "qkT":
                    pe.wait_ge(parts_ready, n // CH + 1)
                    for parts, key in ((q_parts, "qkT"), (k_parts, "qkT1")):
                        bank, full = take(key, n)
                        for h in range(H // 2):
                            h0 = H * (n % CH) + 2 * h
                            mm = pe.transpose(bank.bitcast(F16)[:, P * h:P * (h + 1)],
                                              parts[:, h0:h0 + 2].rearrange("p h s e -> p (h s e)"), ident[:])
                        mm.then_inc(full, 1)
                elif kind in ("att", "att_end"):
                    g = n // STEPS
                    for i in range(4):
                        if i == 2 and n:
                            sums(n - 1)
                        if kind == "att_end":
                            continue
                        if n % STEPS == 0 and i == 0:
                            pe.wait_ge(kz_ready, g + 1)
                        b, qh, hg = group(g)
                        unit = 4 * n + i
                        if unit >= 2:
                            pe.wait_ge(probs_ready, unit - 1)
                        kt = 2 * (n % STEPS) + i // 2
                        for j in range(2):
                            h = 2 * (i % 2) + j
                            mm = pe.matmul(sc_ps[:, unit % 2, j], kz[:, g % 2, h, P * kt:P * (kt + 1)],
                                           qT[:, b, 2 * hg + i % 2, QW * qh:QW * (qh + 1)], start=True, stop=True)
                        mm.then_inc(scores_ready, 1)
                elif kind == "accT":
                    bank, full = take(kind, n)
                    pe.wait_ge(acc_ready, n + 1)
                    for t in range(UNIT_TILES):
                        mm = pe.transpose(bank[:, P * t:P * (t + 1)], accT[:, P * t:P * (t + 1)], identf[:])
                    mm.then_inc(full, 1)
                elif kind == "oT":
                    if n % 2:
                        bank0, n0 = BANK_USE[("oT", n - 1)]
                        pe.wait_ge(bank_free[bank0], n0)
                    bank, full = take(kind, n)
                    for t in range(2):
                        tile = 2 * n + t
                        for k in range(KD):
                            i = KD * t + k
                            mm = pe.transpose(bank[:, P * i:P * (i + 1)],
                                              attn[tile // TB][:, tile % TB, P * k:P * (k + 1)], identf[:])
                    mm.then_inc(full, 1)
                elif kind == "y":
                    if n == 0:
                        pe.wait_ge(ld_o, 16)
                    bank, full = take(kind, n)
                    for t in range(2):
                        for k in range(KD):
                            mm = pe.matmul(bank[:, D * t:D * (t + 1)], tT[:, 2 * (n % 2) + t, k], wo_sb[:, k],
                                           start=(k == 0), stop=(k == KD - 1))
                    mm.then_inc(full, 1)
                elif kind == "u2T":
                    bank, full = take(kind, n)
                    pe.wait_ge(u2_ready, n // 2 + 1)
                    for t in range(2):
                        for k in range(KD):
                            i = KD * t + k
                            mm = pe.transpose(bank[:, P * i:P * (i + 1)], u2[:, 2 * (n % 2) + t, P * k:P * (k + 1)],
                                              identf[:])
                    mm.then_inc(full, 1)
                elif kind == "ff":
                    if n == 0:
                        pe.wait_ge(fold_ready, 1)
                    bank, full = take(kind, n)
                    other, m = BANK_USE[("u2T", 2 * (n // 4) + n % 4 // 2)]
                    pe.wait_ge(bank_free[other], m + 1)
                    for k in range(KD):
                        mm = pe.matmul(bank, tT[:, n % 4, k], fg[:, k], start=(k == 0), stop=(k == KD - 1))
                    mm.then_inc(full, 1)

        @block.vector
        def _(dve):
            count = [0]

            def mark(ins):
                count[0] += 1
                ins.then_inc(dve_chain, 1)

            def link(ins):
                mark(ins)
                dve.wait_ge(dve_chain, count[0])

            def tt(o, a, b, op):
                return dve.tensor_tensor(o, a, b, op)

            def ts(o, a, s1, op1, s2=None, op2=None):
                if op2 is None:
                    return dve.tensor_scalar(o, a, s1, None, op1)
                return dve.tensor_scalar(o, a, s1, s2, op1, op2)

            def stt(o, a, s, b, op1, op2):
                return dve.scalar_tensor_tensor(o, a, s, b, op1, op2)

            def dot(a, b, o):
                link(dve.tensor_tensor_reduce(dump, a, b, 1.0, 0.0, ALU.mult, ALU.add, o))

            def rsqrt(y, a, t):
                link(ts(y.bitcast(I32), a.bitcast(I32), 1, ALU.logical_shift_right))
                link(ts(y.bitcast(I32), y.bitcast(I32), -1.0, ALU.mult, float(0x5F3759DF), ALU.add))
                for _ in range(3):
                    link(tt(t, y, y, ALU.mult))
                    link(stt(t, t, -0.5, a, ALU.mult, ALU.mult))
                    link(stt(y, t, 1.5, y, ALU.add, ALU.mult))

            def atanh(o, n, w):
                om, q, e2, p1, m1, num, den = (small[:, free + 300 + 16 * i:free + 300 + 16 * i + w] for i in range(7))
                link(ts(om, n, -1.0, ALU.mult, 1.0, ALU.add))
                link(dve.reciprocal(q, om))
                link(stt(q, n, 1.0, q, ALU.add, ALU.mult))
                link(ts(e2.bitcast(I32), q.bitcast(I32), 0x7F800000, ALU.bitwise_and))
                mark(ts(p1, e2, 1.0, ALU.add))
                mark(ts(m1, e2, -1.0, ALU.mult, 1.0, ALU.add))
                link(ts(q.bitcast(I32), e2.bitcast(I32), 23, ALU.logical_shift_right))
                mark(tt(num, n, p1, ALU.mult))
                mark(tt(den, n, m1, ALU.mult))
                link(ts(q, q.bitcast(I32), 127.0, ALU.subtract, math.log(2.0) / 2, ALU.mult))
                mark(tt(num, num, m1, ALU.add))
                link(tt(den, den, p1, ALU.add))
                link(dve.reciprocal(den, den))
                link(tt(num, num, den, ALU.mult))
                link(tt(den, num, num, ALU.mult))
                terms = 8
                link(ts(om, den, 1.0 / (2 * terms + 1), ALU.mult))
                for i in range(terms - 1, 0, -1):
                    link(stt(om, om, 1.0 / (2 * i + 1), den, ALU.add, ALU.mult))
                link(stt(om, om, 1.0, num, ALU.add, ALU.mult))
                link(tt(o, om, q, ALU.add))

            def row_norms(st, n2, rstd, w):
                t1, t2, n, s = (small[:, free + 200 + 16 * i:free + 200 + 16 * i + w] for i in range(4))
                mean, var = st[:, :, 0], st[:, :, 1]
                link(tt(t1, mean, mean, ALU.mult))
                link(tt(t1, t1, var, ALU.add))
                link(ts(n2, t1, float(D), ALU.mult))
                link(ts(t1, n2, EPS2, ALU.max))
                rsqrt(t2, t1, n)
                link(tt(n, t1, t2, ALU.mult))
                link(ts(n, n, MAX_TANH, ALU.min))
                atanh(s, n, w)
                link(tt(s, s, t2, ALU.mult))
                link(tt(t1, s, s, ALU.mult))
                link(tt(t1, t1, var, ALU.mult))
                link(ts(t1, t1, 1e-6, ALU.add))
                rsqrt(t2, t1, n)
                link(tt(rstd, s, t2, ALU.mult))

            def clip(r, n2, w, t):
                link(ts(n2, n2, EPS2, ALU.max))
                rsqrt(r, n2, t)
                link(ts(r, r, A, ALU.mult, 1.0, ALU.min))

            UT4 = UNIT_TILES
            sm = [small[:, free + UT4 * i:free + UT4 * (i + 1)] for i in range(40)]
            s1, s2, s3, r1 = sm[0], sm[1], sm[2], sm[3]
            s12, rs12, ts12 = (small[:, free + 2 * UT4 * i:free + 2 * UT4 * (i + 1)] for i in (0, 5, 6))
            r_, r_s2 = sm[10], sm[11]
            n_, al, y2, p_, a_, b_, t_ = sm[14:21]
            st1 = small[:, free + UT4 * 22:free + UT4 * 24].rearrange("p (t s) -> p t s", s=2)
            n2_1, rstd1, r2, usq, d1, d2 = sm[24:30]

            def mobius_norm():
                link(ts(s12, s12, EPS2, ALU.max))
                rsqrt(rs12, s12, ts12)
                link(ts(r_, r_, A, ALU.mult, 1.0, ALU.min))
                link(tt(n_, s2, r_s2, ALU.mult))
                link(tt(n_, n_, r_, ALU.mult))
                ts(tanh_in, n_, EPS, ALU.max).then_inc(norm_ready, 1)

            def mobius_factors(x2, tanhs):
                dve.wait_ge(norm_ready, tanhs)
                link(dve.reciprocal(n_, tanh_in))
                link(tt(n_, n_, r_, ALU.mult))
                dve.wait_ge(tanh_ready, tanhs)
                link(tt(al, tanh_out, n_, ALU.mult))
                mark(tt(y2, al, al, ALU.mult))
                link(stt(p_, s3, 2.0, al, ALU.mult, ALU.mult))
                mark(tt(y2, y2, s2, ALU.mult))
                link(ts(p_, p_, 1.0, ALU.add))
                mark(tt(a_, p_, y2, ALU.add))
                mark(ts(b_, x2, -1.0, ALU.mult, 1.0, ALU.add))
                link(tt(t_, x2, y2, ALU.mult))
                mark(tt(b_, b_, al, ALU.mult))
                link(tt(t_, t_, p_, ALU.add))
                link(ts(t_, t_, EPS, ALU.max))
                link(dve.reciprocal(t_, t_))
                mark(tt(a_, a_, t_, ALU.mult))
                link(tt(b_, b_, t_, ALU.mult))

            def full(*key):
                bank, n = BANK_USE[key]
                dve.wait_ge(bank_full[bank], n + 1)
                return wk_ps[:, bank], bank_free[bank]

            pass
            dve.wait_ge(ld_cond, 16)
            for k in range(KD):
                for b in range(B):
                    last = dve.tensor_copy(condB[:, k, b], cond_sb[:, k, b:b + 1].to_broadcast([P, P]))
            last.then_inc(cond_ready, 1)
            for i in range(2):
                dve.wait_ge(ld_x[i], 16)
                for t in range(4 * i, 4 * i + 4):
                    link(dve.bn_stats(bn[:, 0:6], x_sb[:, t]))
                    link(dve.bn_aggr(stats[:, t], bn[:, 0:6]))
            row_norms(stats[:, 0:TB], x_n2[:, 0:TB], x_rstd[:, 0:TB], TB)
            tanhs = 0

            for kind, n in TIMELINE:
                if kind == "ada":
                    dve.wait_ge(ld_bada, 16)
                    for part in (SC1, SC2):
                        link(ts(bada_sb[:, D * part:D * (part + 1)], bada_sb[:, D * part:D * (part + 1)], 1.0, ALU.add))
                    for b in range(B):
                        for i in range(3):
                            bank = (sc_ps[:, 0, 0], sc_ps[:, 0, 1], sc_ps[:, 1, 0],
                                    sc_ps[:, 1, 1], acc_ps[:, 0], acc_ps[:, 1])[3 * b + i]
                            dve.wait_ge(ada_done, 3 * b + i + 1)
                            last = tt(mods[:, b, 2 * i:2 * i + 2].rearrange("p m d -> p (m d)"), bank,
                                      bada_sb[:, 512 * i:512 * (i + 1)], ALU.add)
                            last.then_inc(ada_free, 1)
                    dve.wait_ge(ada_free, 6)
                    link(dve.memset(kz[:, 1].bitcast(F32), 0.0))
                elif kind == "fold":
                    dve.wait_ge(ld_b1, 16)
                    link(dve.tensor_tensor_reduce(sq[:, 0:FF], b1_sb, b1_sb, 1.0, 0.0, ALU.mult, ALU.add, b1_n2))
                    dve.wait_ge(ld_b1c, 16)
                    for half in range(2):
                        if half == 0:
                            for i in range(4):
                                dve.wait_ge(w1T_done, i + 1)
                                dve.tensor_copy(w2w1[:, 2 * i:2 * i + 2, D:2 * D],
                                                sc_ps[:, i // 2, i % 2].rearrange("p (f d) -> p f d", d=D)
                                                ).then_inc(w1T_ready, 1)
                        else:
                            dve.wait_ge(b1B_used, 1)
                        for f in range(4):
                            f8 = 4 * half + f
                            last = dve.tensor_copy(b1cB[:, P * f:P * (f + 1)], b1c_sb[:, f8:f8 + 1].to_broadcast([P, P]))
                        last.then_inc(b1B_ready, 1)
                    for m in range(KD):
                        dve.wait_ge(fold_done, m + 1)
                        mark(dve.tensor_copy(fg[:, m], acc_ps[:, m]))
                    dve.wait_ge(b1B_used, 2)
                    dve.tensor_copy(fg_row[:], sc_ps[:, 0, 0]).then_inc(fold_ready, 1)
                    dve.wait_ge(fold_ready, 1)
                    link(dve.memset(acc_ps[:], 0.0))
                    for i in range(2, 4):
                        dve.wait_ge(ld_x[i], 16)
                        for t in range(4 * i, 4 * i + 4):
                            link(dve.bn_stats(bn[:, 0:6], x_sb[:, t]))
                            link(dve.bn_aggr(stats[:, t], bn[:, 0:6]))
                    row_norms(stats[:, TB:], x_n2[:, TB:], x_rstd[:, TB:], TB)
                elif kind == "u":
                    usq2, ru = small[:, free:free + 2], small[:, free + 2:free + 4]
                    for t in range(CH):
                        tile = CH * n + t
                        b = tile // TB
                        link(stt(u[:, t], x_sb[:, tile], stats[:, tile, 0:1], mods[:, b, SC1], ALU.subtract, ALU.mult))
                        last = stt(u[:, t], u[:, t], x_rstd[:, tile:tile + 1], mods[:, b, SH1], ALU.mult, ALU.add)
                        if t < CH - 1:
                            mark(last)
                    last.then_inc(u_ready, 1)
                    dve.wait_ge(u_ready, n + 1)
                    for t in range(CH):
                        link(dve.tensor_tensor_reduce(z[:, 0, 0:D], u[:, t], u[:, t], 1.0, 0.0, ALU.mult, ALU.add,
                                                      usq2[:, t:t + 1]))
                    clip(ru, usq2, CH, small[:, free + 4:free + 6])
                elif kind == "uT":
                    bank, freed = full(kind, n)
                    dve.tensor_copy(uT.rearrange("p t k m -> p (t k m)"), bank).then_inc(freed, 1)
                elif kind in ("za", "zb"):
                    if n == 0:
                        dve.wait_ge(ld_bqkv, 16)
                    t = int(kind == "zb")
                    bank, freed = full(kind, n)
                    stt(z[:, t, 0:2 * D], bank, ru[:, t:t + 1], bqkv_sb[:, 0:2 * D], ALU.mult, ALU.add).then_inc(freed, 1)
                    if kind == "za":
                        bank, freed = full("za1", n)
                        for t in range(CH):
                            last = stt(z[:, t, 2 * D:3 * D], bank[:, D * t:D * (t + 1)], ru[:, t:t + 1],
                                       bqkv_sb[:, 2 * D:3 * D], ALU.mult, ALU.add)
                        last.then_inc(freed, 1)
                elif kind == "split":
                    bank, m = BANK_USE[("zb", n)]
                    dve.wait_ge(bank_free[bank], m + 1)
                    w = CH * 3 * (H + 1)
                    ss, rn, tmp = (small[:, free + 8 + w * i:free + 8 + w * (i + 1)] for i in range(3))
                    nh = CH * 3 * H
                    zf = z.rearrange("p t n -> p (t n)")
                    link(tt(sq, zf, zf, ALU.mult))
                    link(dve.tensor_reduce(ss[:, 0:nh], sq.rearrange("p (h e) -> p h e", e=HD), AX_X, ALU.add))
                    link(dve.tensor_reduce(ss[:, nh:w], ss[:, 0:nh].rearrange("p (s h) -> p s h", h=H), AX_X, ALU.add))
                    link(ts(ss, ss, EPS2, ALU.max))
                    rsqrt(rn, ss, tmp)
                    link(ts(rn[:, nh:w], rn[:, nh:w], C * A, ALU.mult, C, ALU.min))
                    f = ss[:, 0:nh].rearrange("p (s h) -> p s h", h=H)
                    link(stt(f, rn[:, 0:nh].rearrange("p (s h) -> p s h", h=H), A,
                             rn[:, nh:w].unsqueeze(2).to_broadcast([P, CH * 3, H]), ALU.mult, ALU.min))
                    f4 = ss[:, 0:nh].rearrange("p (t h) -> p t h", t=CH)
                    for t in range(CH):
                        zq = z[:, t, 0:2 * D].rearrange("p (h e) -> p h e", e=HD)
                        mark(tt(zq, zq, f4[:, t, 0:2 * H].unsqueeze(2).to_broadcast([P, 2 * H, HD]), ALU.mult))
                    for t in range(CH):
                        link(tt(v1[:, CH * n + t, :, 0:HD], z[:, t, 2 * D:3 * D].rearrange("p (h e) -> p h e", e=HD),
                                f4[:, t, 2 * H:3 * H].unsqueeze(2).to_broadcast([P, H, HD]), ALU.mult))
                    for s, parts, lo in ((0, q_parts, 2), (1, k_parts, 1)):
                        for t in range(CH):
                            zz = z[:, t, D * s:D * (s + 1)].rearrange("p (h e) -> p h e", e=HD)
                            pt = parts[:, H * t:H * (t + 1)]
                            link(dve.tensor_copy(pt[:, :, 0], zz))
                            link(tt(pt[:, :, lo], zz, pt[:, :, 0], ALU.subtract))
                    mark(dve.tensor_copy(q_parts[:, :, 1], q_parts[:, :, 0]))
                    mark(dve.tensor_copy(q_parts[:, :, 3], q_parts[:, :, 2]))
                    dve.tensor_copy(k_parts[:, :, 2:4], k_parts[:, :, 0:2]).then_inc(parts_ready, 1)
                elif kind == "qkT":
                    b, t = n // TB, n % TB
                    for key, dst in (("qkT", qT), ("qkT1", kT)):
                        bank, freed = full(key, n)
                        dve.tensor_copy(dst[:, b, :, P * t:P * (t + 1)],
                                        bank.bitcast(F16).rearrange("p (h m) -> p h m", m=P)).then_inc(freed, 1)
                elif kind == "stage":
                    b, _, hg = group(n)
                    if n == 0:
                        dve.wait_ge(idents, 4)
                    if n >= 2:
                        dve.wait_ge(sums_done, STEPS * (n - 1))
                    last_tile = TB * (b + 1) - 1
                    bank, m = BANK_USE[("qkT1", last_tile)]
                    dve.wait_ge(bank_free[bank], m + 1)
                    for odd in range(2):
                        rows = slice(64 * odd, 64 * odd + 64)
                        last = dve.tensor_copy(kz[rows, n % 2, odd::2], kT[rows, b, 2 * hg:2 * hg + 2])
                    last.then_inc(kz_ready, 1)
                elif kind == "acc":
                    dve.wait_ge(sums_done, STEPS * (n + 1))
                    if n:
                        bank, m = BANK_USE[("accT", n - 1)]
                        dve.wait_ge(bank_full[bank], m + 1)
                    dve.tensor_copy(accT[:], acc_ps[:, n % 2]).then_inc(acc_ready, 1)
                elif kind == "accT":
                    b, qh, hg = group(n)
                    bank, freed = full(kind, n)
                    rows = bank.rearrange("p (t h e) -> p t h e", h=HG, e=32)
                    rden = small[:, free + 400:free + 400 + UNIT_TILES * HG].rearrange("p (t h) -> p t h", h=HG)
                    link(dve.reciprocal(rden, rows[:, :, :, HD]))
                    o = attn[b][:, UNIT_TILES * qh:UNIT_TILES * (qh + 1), HG * HD * hg:HG * HD * (hg + 1)]
                    tt(o.rearrange("p t (h e) -> p t h e", e=HD), rows[:, :, :, 0:HD],
                       rden.unsqueeze(3).to_broadcast([P, UNIT_TILES, HG, HD]), ALU.mult).then_inc(freed, 1)
                elif kind in ("oT", "u2T"):
                    if kind == "oT" and n % 2 == 0 and n >= 2:
                        dve.wait_ge(stored, 16 * (n // 2))
                    bank, freed = full(kind, n)
                    dve.tensor_copy(tT[:, 2 * (n % 2):2 * (n % 2) + 2].rearrange("p t k m -> p (t k m)"), bank
                                    ).then_inc(freed, 1)
                elif kind == "y":
                    if n == 0:
                        dve.wait_ge(ld_bo, 16)
                    bank, freed = full(kind, n)
                    for t in range(2):
                        last = stt(y_sb[:, 2 * (n % 2) + t], bank[:, D * t:D * (t + 1)], 1.0 / C, bo_sb[:], ALU.mult, ALU.add)
                        if t == 0:
                            mark(last)
                    last.then_inc(freed, 1)
                elif kind in ("mid", "end"):
                    b = UNIT_TILES * n // TB
                    g_part = G1 if kind == "mid" else G2
                    if kind == "mid":
                        bank, m = BANK_USE[("y", 2 * n + 1)]
                        dve.wait_ge(bank_free[bank], m + 1)
                        base = x_sb[:, UNIT_TILES * n:UNIT_TILES * (n + 1)]
                    else:
                        base = x1
                        for t in range(UT4):
                            dot(u2[:, t], fg_row[:, D:2 * D], d2[:, t:t + 1])
                        link(tt(t_, r2, r2, ALU.mult))
                        link(tt(d1, d1, t_, ALU.mult))
                        link(tt(d2, d2, r2, ALU.mult))
                        link(stt(d1, d2, 2.0, d1, ALU.mult, ALU.add))
                        link(ts(d1, d1, b1_n2, ALU.add))
                        clip(r1, d1, UT4, t_)
                        link(tt(r2, r1, r2, ALU.mult))
                        if n == 0:
                            dve.wait_ge(ld_b2, 16)
                        for t in range(UT4):
                            link(stt(dump, fg_row[:, 0:D], r1[:, t:t + 1], b2_sb[:], ALU.mult, ALU.add))
                            link(stt(y_sb[:, t], y_sb[:, t], r2[:, t:t + 1], dump, ALU.mult, ALU.add))
                    for t in range(UT4):
                        dot(y_sb[:, t], y_sb[:, t], s1[:, t:t + 1])
                    link(tt(y_sb, y_sb, mods[:, b, g_part].unsqueeze(1).to_broadcast([P, UT4, D]), ALU.mult))
                    for t in range(UT4):
                        dot(y_sb[:, t], y_sb[:, t], s2[:, t:t + 1])
                        dot(y_sb[:, t], base[:, t], s3[:, t:t + 1])
                    mobius_norm()
                elif kind == "mid_tanh":
                    tanhs += 1
                    tiles = slice(UNIT_TILES * n, UNIT_TILES * (n + 1))
                    b = UNIT_TILES * n // TB
                    mobius_factors(x_n2[:, tiles], tanhs)
                    for t in range(UT4):
                        link(ts(x1[:, t], x_sb[:, UT4 * n + t], a_[:, t:t + 1], ALU.mult))
                        link(stt(x1[:, t], y_sb[:, t], b_[:, t:t + 1], x1[:, t], ALU.mult, ALU.add))
                    for t in range(UT4):
                        link(dve.bn_stats(bn[:, 0:6], x1[:, t]))
                        link(dve.bn_aggr(st1[:, t], bn[:, 0:6]))
                    row_norms(st1, n2_1, rstd1, UT4)
                    for t in range(UT4):
                        link(stt(u2[:, t], x1[:, t], st1[:, t, 0:1], mods[:, b, SC2], ALU.subtract, ALU.mult))
                        last = stt(u2[:, t], u2[:, t], rstd1[:, t:t + 1], mods[:, b, SH2], ALU.mult, ALU.add)
                        if t < UT4 - 1:
                            mark(last)
                    last.then_inc(u2_ready, 1)
                    dve.wait_ge(u2_ready, n + 1)
                    for t in range(UT4):
                        dot(u2[:, t], u2[:, t], usq[:, t:t + 1])
                    clip(r2, usq, UT4, t_)
                elif kind == "ff":
                    bank, freed = full(kind, n)
                    t = n % UT4
                    mark(dve.tensor_copy(y_sb[:, t], bank[:, 0:D]))
                    dve.tensor_tensor_reduce(dump, u2[:, t], bank[:, D:2 * D], 1.0, 0.0, ALU.mult, ALU.add,
                                             d1[:, t:t + 1]).then_inc(freed, 1)
                    bank, m = BANK_USE[(kind, n)]
                    dve.wait_ge(bank_free[bank], m + 1)
                elif kind == "end_tanh":
                    tanhs += 1
                    mobius_factors(n2_1, tanhs)
                    for t in range(UT4):
                        link(stt(x1[:, t], x1[:, t], a_[:, t:t + 1], x_sb[:, UT4 * n + t], ALU.mult, ALU.add))
                        last = stt(u2[:, t], y_sb[:, t], b_[:, t:t + 1], x1[:, t], ALU.mult, ALU.add)
                        if t < UT4 - 1:
                            mark(last)
                    last.then_inc(out_ready, 1)




def kernel(x, cond_1024, L0_cond_w_q, L0_cond_b_q, L0_cond_w_k, L0_cond_b_k, L0_cond_w_v, L0_cond_b_v,
           L0_cond_w_o, L0_cond_b_o, L0_cond_w_f1, L0_cond_b_f1, L0_cond_w_f2, L0_cond_b_f2,
           L0_cond_w_ada, L0_cond_b_ada):
    import concourse.bacc as bacc
    from concourse.bass_utils import run_bass_kernel_spmd

    def rows(w):
        w = np.asarray(w)
        return np.ascontiguousarray(w.reshape(-1, P, w.shape[-1]).transpose(1, 0, 2))

    w_qkv = np.concatenate([np.asarray(w) for w in (L0_cond_w_q, L0_cond_w_k, L0_cond_w_v)], axis=1)
    b_qkv = np.concatenate([np.asarray(b) for b in (L0_cond_b_q, L0_cond_b_k, L0_cond_b_v)])
    b1 = np.asarray(L0_cond_b_f1)
    arrays = {
        "in_x": rows(np.asarray(x).reshape(B * S, D)),
        "in_cond_t": rows(np.ascontiguousarray(np.asarray(cond_1024).T)),
        "in_w_ada": rows(L0_cond_w_ada), "in_b_ada": np.asarray(L0_cond_b_ada),
        "in_w_qkv": rows(w_qkv), "in_b_qkv": b_qkv,
        "in_w_o": rows(L0_cond_w_o), "in_b_o": np.asarray(L0_cond_b_o),
        "in_w_f1": rows(L0_cond_w_f1), "in_b_f1": b1,
        "in_b_f1_cols": np.ascontiguousarray(b1.reshape(KF, P).T),
        "in_w_f2": rows(L0_cond_w_f2), "in_b_f2": np.asarray(L0_cond_b_f2),
    }
    nc = bacc.Bacc("TRN2", target_bir_lowering=False, num_devices=1)
    ap = {k: nc.dram_tensor(k, a.shape, mybir.dt.from_np(a.dtype), kind="ExternalInput").ap()
          for k, a in arrays.items()}
    out = nc.dram_tensor("out_x", (P, TILES, D), F32, kind="ExternalOutput").ap()
    build(nc, ap["in_x"], ap["in_cond_t"], ap["in_w_ada"], ap["in_b_ada"], ap["in_w_qkv"], ap["in_b_qkv"],
          ap["in_w_o"], ap["in_b_o"], ap["in_w_f1"], (ap["in_b_f1"], ap["in_b_f1_cols"]), ap["in_w_f2"],
          ap["in_b_f2"], out)
    got = run_bass_kernel_spmd(nc, [arrays], core_ids=[0]).results[0]["out_x"]
    return got.transpose(1, 0, 2).reshape(B, S, D)
```

```python
import math
from contextlib import ExitStack

import numpy as np

import concourse.bass as bass
from concourse import mybir

F32 = mybir.dt.float32
F16 = mybir.dt.float16
I32 = mybir.dt.int32
ALU = mybir.AluOpType
ACT = mybir.ActivationFunctionType
AX_X = mybir.AxisListType.X

P = 128
B, S, D, H, FF = 2, 1024, 256, 16, 1024
HD = D // H
KD = D // P
KF = FF // P
TILES = B * S // P
TB = TILES // B
CH = 2
HG = 4
RING = 3
QW = 512
GROUPS = B * (S // QW) * (H // HG)
KT = S // P
KTU = 2
UNITS = GROUPS * KT * KTU
UT = QW // P
LAYER_UNITS = TILES // UT

EPS = 1e-7
EPS2 = EPS * EPS
MAX_TANH = float(np.float32(1.0 - 1e-5))
A = math.atanh(MAX_TANH)


def _beta(a, b):
    return math.exp(math.lgamma(a) + math.lgamma(b) - math.lgamma(a + b))


C = _beta(HD / 2, 0.5) / _beta(D / 2, 0.5)
assert C * C > H and A * A / math.sqrt(HD) < 60

SH1, SC1, G1, SH2, SC2, G2 = range(6)


def _atanh_series():
    w = (0.5 - 0.5 * np.cos(np.pi * (np.arange(2000) + 0.5) / 2000)) / 9
    fit = np.polynomial.chebyshev.Chebyshev.fit(w, np.arctanh(np.sqrt(w)) / np.sqrt(w), 4)
    return [float(c) for c in fit.convert(kind=np.polynomial.Polynomial).coef]


ATANH = _atanh_series()


def group(g):
    n = H // HG
    return g // (2 * n), g // n % 2, g % n


def timeline():
    fill = {}

    def put(unit, *jobs):
        for job in jobs:
            fill.setdefault(int(unit), []).append(job)

    out = [("ada", i) for i in range(6)] + [("u_all", 0)]
    chunks = TB // CH
    out += [("uT", 0), ("za", 0), ("zb", 0)]
    fold = [[("foldT", i) for i in range(4)] + [("foldF", 0)], [("foldF", 1)], [("foldB", 0)], []]
    for c in range(chunks):
        out += fold[c]
        out += [("split", c)]
        if c + 1 < chunks:
            out += [("uT", c + 1), ("za", c + 1), ("zb", c + 1)]
        out += [("qkT", 2 * c), ("qkT", 2 * c + 1)]
    out += [("stage", 0), ("sums_zero", 0)]

    put(2, ("x_stats", 1))
    for c, n in zip(range(chunks, 2 * chunks), PROJ_AT):
        put(n, ("u", c))
        put(n + 3, ("u_sq", c))
        put(n + 4, ("uT", c))
        put(n + 6, ("za", c))
        put(n + 8, ("zb", c))
        put(n + 10, ("split", c))
        put(n + 22, ("qkT", 2 * c))
        put(n + 24, ("qkT", 2 * c + 1))

    def layers(v, n, d):
        put(n, ("oT", 2 * v))
        put(n + d, ("oT", 2 * v + 1))
        put(n + 2 * d, ("y", 2 * v))
        put(n + 3 * d, ("y", 2 * v + 1))
        put(n + 3 * d, ("gy", v))
        put(n + 6 * d, ("mid", v))
        put(n + 8 * d, ("mid_tanh", v))
        put(n + 16 * d, ("u2_norm", v))
        put(n + 18 * d, ("u2T", 2 * v))
        put(n + 19 * d, ("u2T", 2 * v + 1))
        for t in range(UT):
            put(n + (20 + 2 * t) * d, ("ff", UT * v + t))
        put(n + 27 * d, ("end", v))
        put(n + 31 * d, ("end_norm", v))
        put(n + 33 * d, ("end_tanh", v))

    for v, n in enumerate(LAYERS_AT):
        layers(v, n, LAYERS_PACE)
    layers(LAYER_UNITS - 1, UNITS + 8, 1)

    per = KT * KTU
    for n in range(UNITS):
        out.append(("exp", n))
        if n % KTU == KTU - 1 and n >= 2 * KTU - 1:
            out.append(("sums", n // KTU - 1))
        g = n // per
        if n % per == 3 and g:
            out.append(("acc", g - 1))
        if n % per == 8 and g + 1 < GROUPS:
            out.append(("stage", g + 1))
        if n % per == 6 and g:
            out.append(("accT", g - 1))
        out += fill.pop(n, [])
    out += [("sums", UNITS // KTU - 1), ("acc", GROUPS - 1), ("accT", GROUPS - 1)]
    for n in sorted(fill):
        out += fill[n]
    return out


PROJ_AT = (12, 40, 67, 92)
LAYERS_AT = (74, 138, 202)
LAYERS_PACE = 1.6
TIMELINE = timeline()

SCORES, SUMS = 2, 6


def bank_of(kind, n):
    early = n < TB // CH if kind in ("zb",) else n < TB
    return {
        "ada": lambda: SCORES + n, "uT": lambda: 0, "za": lambda: 1, "zv": lambda: 0,
        "zb": lambda: SUMS + 1 if early else 1, "foldT": lambda: SUMS, "foldF": lambda: SUMS,
        "foldB": lambda: SUMS, "qT": lambda: SCORES + 2 * (n % 2) if early else 0,
        "kT": lambda: SCORES + 1 + 2 * (n % 2) if early else 1, "accT": lambda: n % 2,
        "oT": lambda: n % 2, "y": lambda: n % 2, "u2T": lambda: n % 2, "ff": lambda: n % 2,
    }[kind]()


def uses_of_banks():
    at, count = {}, [0] * 8
    for kind, n in TIMELINE:
        keys = {"za": ("za", "zv"), "qkT": ("qT", "kT")}.get(kind, (kind,))
        if kind in ("ada", "uT", "za", "zb", "foldT", "foldF", "foldB", "qkT", "accT", "oT", "y", "u2T", "ff"):
            for key in keys:
                bank = bank_of(key, n)
                at[key, n] = (bank, count[bank])
                count[bank] += 1
    return at, count


BANK_USE, BANK_USES = uses_of_banks()
def build(nc, x, cond_t, w_ada, b_ada, w_qkv, b_qkv, w_o, b_o, w_f1, b_f1, b_f1_cols, w_f2, b_f2, out):
    with ExitStack() as ctx:
        def sb(name, shape, dt=F32):
            return ctx.enter_context(nc.sbuf_tensor(name, shape, dt))

        def sem(name):
            return ctx.enter_context(nc.semaphore(name))

        x_sb = sb("x_sb", [P, TILES, D])
        qT = sb("qT", [P, B, H // 2, S], F16)
        kT = sb("kT", [P, B, H // 2, S], F16)
        kz = sb("kz", [P, 2, HG, S], F16)
        v1 = sb("v1", [P, TILES, H, HD + 1])
        probs = sb("probs", [P, RING, HG, QW])
        attn0 = sb("attn0", [P, TB, D])
        accT = sb("accT", [P, QW])
        wo_sb = sb("wo_sb", [P, KD, D])
        fg = sb("fg", [P, KD, 2 * D])
        fg_row = sb("fg_row", [P, 2 * D])
        wqkv_sb = sb("wqkv_sb", [P, KD, 3 * D])
        bqkv_sb = sb("bqkv_sb", [P, 3 * D])
        bo_sb = sb("bo_sb", [P, D])
        b2_sb = sb("b2_sb", [P, D])
        mods = sb("mods", [P, B, 6, D])
        identf = sb("identf", [P, P])
        ident = sb("ident", [P, P], F16)
        proj = sb("proj", [P, 4608])
        lay = sb("lay", [P, 2, UT, D])
        small = sb("small", [P, 664])

        u_two = proj[:, 0:512].rearrange("p (t d) -> p t d", t=CH)
        uT = proj[:, 512:1024].rearrange("p (t k m) -> p t k m", t=CH, k=KD)
        z = proj[:, 1024:2560].rearrange("p (t n) -> p t n", t=CH)
        sq = proj[:, 2560:4096].rearrange("p (t n) -> p t n", t=CH)
        q_parts = proj[:, 2560:3584].bitcast(F16).rearrange("p (h s e) -> p h s e", s=4, e=HD)
        k_parts = proj[:, 3584:4608].bitcast(F16).rearrange("p (h s e) -> p h s e", s=4, e=HD)
        q_used = qT[:].bitcast(F32)[:, 0, :, 0:D]
        y_sb, x1 = q_used[:, 0:UT], q_used[:, UT:2 * UT]
        u2 = lay[:, 0]
        tT = lay[:, 1].rearrange("p t (k m) -> p t k m", k=KD)
        gz = lay[:, 1]
        pr = probs[:].rearrange("p r h q -> p (r h q)")
        w2w1 = pr[:, 0:4096].rearrange("p (f n) -> p f n", f=KF)
        b1_sb = pr[:, 4096:4096 + FF]
        ada_sb = qT[:, 1].rearrange("p h s -> p (h s)").bitcast(F32)[:, 0:3072].rearrange("p (k n) -> p k n", k=KD)
        k_later = kT[:, 1].rearrange("p h s -> p (h s)").bitcast(F32)
        u_batch = k_later[:, 0:TB * D].rearrange("p (t d) -> p t d", d=D)
        bada_sb = k_later[:, TB * D:TB * D + 6 * D]
        w1_sb = attn0[:].rearrange("p t d -> p (t d)").rearrange("p (k n) -> p k n", k=KD)
        attn1 = kT[:, 0].rearrange("p h s -> p (h s)").bitcast(F32)[:, 0:TB * D].rearrange("p (t d) -> p t d", d=D)
        attn = [attn0[:], attn1]

        dump = mods[:, 0, SH1:SC1 + 1]

        def u_of(c):
            return u_batch[:, CH * c:CH * (c + 1)] if CH * c < TB else u_two

        at = [0]

        def cols(n):
            at[0] += n
            return small[:, at[0] - n:at[0]]

        stats = cols(2 * TILES).rearrange("p (t s) -> p t s", s=2)
        x_n2, x_rstd, b1_n2 = cols(TILES), cols(TILES), cols(1)
        cols(1)
        cond_sb = cols(KD * B).rearrange("p (k b) -> p k b", k=KD)
        b1c_sb = cols(KF)
        bn = cols(6 * TB).rearrange("p (t s) -> p t s", s=6)
        rowt = [cols(TB) for _ in range(11)]
        usq, ru, clip_t = cols(TB), cols(TB), cols(TB)
        W3 = CH * 3 * (H + 1)
        ss, rn, split_t = cols(W3), cols(W3), cols(W3)
        rden = cols(UT * HG).rearrange("p (t h) -> p t h", h=HG)
        s12, rs12, ts12 = cols(2 * UT), cols(2 * UT), cols(2 * UT)
        s1, s2, r_, r_s2 = s12[:, 0:UT], s12[:, UT:], rs12[:, 0:UT], rs12[:, UT:]
        s3, n_, al, y2, p_, a_, b_, t_, n2_1, rstd1, r2, usq2, d1, d2, r1 = (cols(UT) for _ in range(15))
        tanh_in, tanh_out = cols(UT), cols(UT)
        st1 = cols(2 * UT).rearrange("p (t s) -> p t s", s=2)

        wk_ps = ctx.enter_context(nc.psum_tensor("wk_ps", [P, 2, 512], F32))
        sc_ps = ctx.enter_context(nc.psum_tensor("sc_ps", [P, 2, 2, QW], F32))
        acc_ps = ctx.enter_context(nc.psum_tensor("acc_ps", [P, 2, QW], F32))
        banks = [wk_ps[:, 0], wk_ps[:, 1], sc_ps[:, 0, 0], sc_ps[:, 0, 1], sc_ps[:, 1, 0], sc_ps[:, 1, 1],
                 acc_ps[:, 0], acc_ps[:, 1]]

        ld_x = [sem(f"ld_x{i}") for i in range(4)]
        ld_cond, ld_ada, ld_bada = sem("ld_cond"), sem("ld_ada"), sem("ld_bada")
        ld_qkv, ld_bqkv, ld_o, ld_bo = sem("ld_qkv"), sem("ld_bqkv"), sem("ld_o"), sem("ld_bo")
        ld_f1, ld_f2, ld_b1, ld_b1c, ld_b2 = sem("ld_f1"), sem("ld_f2"), sem("ld_b1"), sem("ld_b1c"), sem("ld_b2")
        consts = sem("consts")
        bank_full = [sem(f"bank{i}_full") for i in range(8)]
        bank_free = [sem(f"bank{i}_free") for i in range(8)]
        u_ready = sem("u_ready")
        usq_ready = sem("usq_ready")
        z_ready = sem("z_ready")
        zsq_ready = sem("zsq_ready")
        parts_ready = sem("parts_ready")
        kz_ready = sem("kz_ready")
        sums_zeroed = sem("sums_zeroed")
        scores_ready = sem("scores_ready")
        probs_ready = sem("probs_ready")
        sums_done = sem("sums_done")
        acc_ready = sem("acc_ready")
        gy_ready = sem("gy_ready")
        ysq_ready = sem("ysq_ready")
        u2_ready, u2sq_ready = sem("u2_ready"), sem("u2sq_ready")
        norm_ready, tanh_ready = sem("norm_ready"), sem("tanh_ready")
        out_ready, stored = sem("out_ready"), sem("stored")
        b1sq_ready = sem("b1sq_ready")
        dve_chain, pool_chain, act_chain = sem("dve_chain"), sem("pool_chain"), sem("act_chain")

        block = ctx.enter_context(nc.Block())

        @block.sync
        def _(sp):
            sp.dma_start(cond_sb, cond_t).then_inc(ld_cond, 16)
            for i in range(2):
                sp.dma_start(x_sb[:, 4 * i:4 * i + 4], x[:, 4 * i:4 * i + 4]).then_inc(ld_x[i], 16)
            sp.dma_start(ada_sb, w_ada).then_inc(ld_ada, 16)
            sp.dma_start(wqkv_sb[:], w_qkv).then_inc(ld_qkv, 16)
            sp.dma_start(w1_sb, w_f1).then_inc(ld_f1, 16)
            sp.dma_start(w2w1[:, :, 0:D], w_f2).then_inc(ld_f2, 16)
            for i in range(2, 4):
                sp.dma_start(x_sb[:, 4 * i:4 * i + 4], x[:, 4 * i:4 * i + 4]).then_inc(ld_x[i], 16)
            sp.dma_start(wo_sb[:], w_o).then_inc(ld_o, 16)
            for v in range(LAYER_UNITS):
                sp.wait_ge(out_ready, v + 1)
                sp.dma_start(out[:, UT * v:UT * (v + 1)], u2).then_inc(stored, 16)
            sp.wait_ge(stored, 16 * LAYER_UNITS)

        @block.gpsimd
        def _(pool):
            n = 0
            for t in (identf, ident):
                pool.memset(t[:], 0.0).then_inc(pool_chain, 1)
                n += 1
                pool.wait_ge(pool_chain, n)
                pool.affine_select(out=t[:], in_=t[:], compare_op=ALU.not_equal, fill=1.0, base=0,
                                   pattern=[[-1, P]], channel_multiplier=1).then_inc(consts, 1)
            pool.memset(v1[:, :, :, HD:HD + 1], 1.0).then_inc(consts, 1)
            pool.memset(kz[:].bitcast(F32), 0.0).then_inc(consts, 1)

        def full(eng, key, n):
            bank, use = BANK_USE[key, n]
            eng.wait_ge(bank_full[bank], use + 1)
            return banks[bank], bank_free[bank]

        def drained(eng, key, n):
            bank, use = BANK_USE[key, n]
            eng.wait_ge(bank_free[bank], use + 1)

        @block.scalar
        def _(act):
            act.dma_start(bada_sb, b_ada.partition_broadcast(P)).then_inc(ld_bada, 16)
            act.dma_start(bqkv_sb[:], b_qkv.partition_broadcast(P)).then_inc(ld_bqkv, 16)
            act.dma_start(b1c_sb, b_f1_cols).then_inc(ld_b1c, 16)
            act.dma_start(b1_sb, b_f1.partition_broadcast(P)).then_inc(ld_b1, 16)
            act.dma_start(bo_sb[:], b_o.partition_broadcast(P)).then_inc(ld_bo, 16)
            act.dma_start(b2_sb[:], b_f2.partition_broadcast(P)).then_inc(ld_b2, 16)

            def square(a, junk, total):
                return act.activation(junk, a, ACT.Square, accum_out=total)

            def copy(o, key, n):
                bank, freed = full(act, key, n)
                if o.dtype == F16:
                    bank = bank.bitcast(F16)
                if len(o.shape) == 3:
                    bank = bank.rearrange("p (h m) -> p h m", m=o.shape[2])
                act.activation(o, bank, ACT.Copy).then_inc(freed, 1)

            chain = 0
            tanhs = 0
            for kind, n in TIMELINE:
                if kind == "u_all":
                    for t in range(TB):
                        act.wait_ge(u_ready, t + 1)
                        square(u_batch[:, t], lay[:, t // UT, t % UT], usq[:, t:t + 1]).then_inc(usq_ready, 1)
                elif kind == "u_sq":
                    act.wait_ge(u_ready, CH * (n + 1))
                    for t in range(CH):
                        square(u_two[:, t], sq[:, 0, D * t:D * (t + 1)], usq[:, t:t + 1]).then_inc(usq_ready, 1)
                elif kind == "uT" and CH * n < TB:
                    copy(uT.rearrange("p t k m -> p (t k m)"), kind, n)
                elif kind == "foldT":
                    copy(w2w1[:, 2 * n:2 * n + 2, D:2 * D], kind, n)
                elif kind == "foldF":
                    copy(fg[:, n], kind, n)
                elif kind == "foldB":
                    copy(fg_row[:], kind, n)
                    act.wait_ge(ld_b1, 16)
                    square(b1_sb, b1_sb, b1_n2).then_inc(b1sq_ready, 1)
                elif kind == "split":
                    for t in range(CH):
                        act.wait_ge(z_ready, CH * n + t + 1)
                        act.activation(sq[:, t], z[:, t], ACT.Square).then_inc(zsq_ready, 1)
                elif kind == "qkT" and n < TB:
                    copy(kT[:, 0, :, P * n:P * (n + 1)], "kT", n)
                    copy(qT[:, 0, :, P * n:P * (n + 1)], "qT", n)
                elif kind == "exp":
                    kt = n // KTU
                    act.wait_ge(scores_ready, n + 1)
                    if n % KTU == 0 and kt >= RING:
                        act.wait_ge(sums_done, kt - RING + 1)
                    act.activation(probs[:, kt % RING, 2 * (n % 2):2 * (n % 2) + 2], sc_ps[:, n % 2],
                                   ACT.Exp, scale=1.0 / math.sqrt(HD)).then_inc(probs_ready, 1)
                elif kind == "mid":
                    act.wait_ge(gy_ready, 2 * n + 1)
                    if n:
                        act.wait_ge(stored, 16 * n)
                    for i, (a, total) in enumerate(((y_sb, s1), (x1, s2))):
                        for t in range(UT):
                            last = square(a[:, t], (u2, gz)[i][:, t], total[:, t:t + 1])
                    last.then_inc(ysq_ready, 1)
                elif kind == "u2_norm":
                    act.wait_ge(u2_ready, n + 1)
                    for t in range(UT):
                        last = square(u2[:, t], gz[:, t], usq2[:, t:t + 1])
                    last.then_inc(u2sq_ready, 1)
                elif kind == "end_norm":
                    act.wait_ge(gy_ready, 2 * n + 2)
                    for i, (a, total) in enumerate(((y_sb, s1), (gz, s2))):
                        for t in range(UT):
                            if i:
                                act.wait_ge(act_chain, chain - UT + 1 + t)
                            last = square(a[:, t], u2[:, t], total[:, t:t + 1])
                            if not i:
                                last.then_inc(act_chain, 1)
                                chain += 1
                    last.then_inc(ysq_ready, 1)
                elif kind in ("mid_tanh", "end_tanh"):
                    tanhs += 1
                    act.wait_ge(norm_ready, tanhs)
                    act.activation(tanh_out, tanh_in, ACT.Tanh).then_inc(tanh_ready, 1)

        @block.tensor
        def _(pe):
            def take(key, n):
                bank, use = BANK_USE[key, n]
                if use:
                    pe.wait_ge(bank_free[bank], use)
                return banks[bank], bank_full[bank]

            def product(o, lhs, rhs):
                for k in range(KD):
                    mm = pe.matmul(o, lhs(k), rhs(k), start=(k == 0), stop=(k == KD - 1))
                return mm

            def turn(bank, tiles):
                i = 0
                for tile in tiles:
                    for k in range(KD):
                        mm = pe.transpose(bank[:, P * i:P * (i + 1)], tile[:, P * k:P * (k + 1)], identf[:])
                        i += 1
                return mm

            for kind, n in TIMELINE:
                if kind == "ada":
                    if n == 0:
                        pe.wait_ge(ld_cond, 16)
                        pe.wait_ge(ld_ada, 16)
                    bank, filled = take(kind, n)
                    product(bank, lambda k: cond_sb[:, k, n // 3:n // 3 + 1].to_broadcast([P, P]),
                            lambda k: ada_sb[:, k, 512 * (n % 3):512 * (n % 3 + 1)]).then_inc(filled, 1)
                elif kind == "foldT":
                    if n == 0:
                        pe.wait_ge(ld_f1, 16)
                    bank, filled = take(kind, n)
                    for f in range(2 * n, 2 * n + 2):
                        for k in range(KD):
                            i = 2 * (f % 2) + k
                            mm = pe.transpose(bank[:, P * i:P * (i + 1)], w1_sb[:, k, P * f:P * (f + 1)], identf[:])
                    mm.then_inc(filled, 1)
                elif kind in ("foldF", "foldB"):
                    bank, filled = take(kind, n)
                    if n == 0:
                        pe.wait_ge(ld_f2, 16)
                        pe.wait_ge(ld_b1c, 16)
                    for f in range(KF):
                        lhs = (w2w1[:, f, D + P * n:D + P * (n + 1)] if kind == "foldF"
                               else b1c_sb[:, f:f + 1].to_broadcast([P, P]))
                        mm = pe.matmul(bank, lhs, w2w1[:, f], start=(f == 0), stop=(f == KF - 1))
                    mm.then_inc(filled, 1)
                elif kind == "uT":
                    bank, filled = take(kind, n)
                    pe.wait_ge(u_ready, CH * (n + 1))
                    if n == 0:
                        pe.wait_ge(consts, 4)
                    turn(bank, [u_of(n)[:, t] for t in range(CH)]).then_inc(filled, 1)
                elif kind == "za":
                    if n == 0:
                        pe.wait_ge(ld_qkv, 16)
                    drained(pe, "uT", n)
                    bank, filled = take("za", n)
                    product(bank, lambda k: uT[:, 0, k], lambda k: wqkv_sb[:, k, 0:2 * D]).then_inc(filled, 1)
                    bank, filled = take("zv", n)
                    for t in range(CH):
                        mm = product(bank[:, D * t:D * (t + 1)], lambda k: uT[:, t, k],
                                     lambda k: wqkv_sb[:, k, 2 * D:3 * D])
                    mm.then_inc(filled, 1)
                elif kind == "zb":
                    bank, filled = take("zb", n)
                    product(bank, lambda k: uT[:, 1, k], lambda k: wqkv_sb[:, k, 0:2 * D]).then_inc(filled, 1)
                elif kind == "qkT":
                    pe.wait_ge(parts_ready, n // CH + 1)
                    for parts, key in ((k_parts, "kT"), (q_parts, "qT")):
                        bank, filled = take(key, n)
                        for h in range(H // 2):
                            h0 = H * (n % CH) + 2 * h
                            mm = pe.transpose(bank.bitcast(F16)[:, P * h:P * (h + 1)],
                                              parts[:, h0:h0 + 2].rearrange("p h s e -> p (h s e)"), ident[:])
                        mm.then_inc(filled, 1)
                elif kind == "exp":
                    g, kt = n // (KT * KTU), n // KTU % KT
                    b, qh, hg = group(g)
                    if n == 0:
                        for i in range(SCORES, SUMS):
                            pe.wait_ge(bank_free[i], BANK_USES[i])
                    if n % (KT * KTU) == 0:
                        pe.wait_ge(kz_ready, g + 1)
                    if n >= 2:
                        pe.wait_ge(probs_ready, n - 1)
                    for j in range(2):
                        mm = pe.matmul(sc_ps[:, n % 2, j], kz[:, g % 2, 2 * (n % 2) + j, P * kt:P * (kt + 1)],
                                       qT[:, b, 2 * hg + n % 2, QW * qh:QW * (qh + 1)], start=True, stop=True)
                    mm.then_inc(scores_ready, 1)
                elif kind == "sums":
                    g, kt = n // KT, n % KT
                    b, _, hg = group(g)
                    pe.wait_ge(probs_ready, KTU * (n + 1))
                    if n == 0:
                        pe.wait_ge(sums_zeroed, 1)
                    if kt == 0 and g >= 2:
                        pe.wait_ge(acc_ready, g - 1)
                    for j in range(HG):
                        mm = pe.matmul(acc_ps[32 * j:32 * j + HD + 1, g % 2], v1[:, TB * b + kt, HG * hg + j],
                                       probs[:, n % RING, j], start=(kt == 0), stop=(kt == KT - 1),
                                       tile_position=(0, 32 * j))
                    mm.then_inc(sums_done, 1)
                elif kind == "accT":
                    bank, filled = take(kind, n)
                    pe.wait_ge(acc_ready, n + 1)
                    for t in range(UT):
                        mm = pe.transpose(bank[:, P * t:P * (t + 1)], accT[:, P * t:P * (t + 1)], identf[:])
                    mm.then_inc(filled, 1)
                elif kind == "oT":
                    drained(pe, "accT", (H // HG) * (n // 2 + 1) - 1)
                    bank, filled = take(kind, n)
                    turn(bank, [attn[2 * n // TB][:, (2 * n + t) % TB] for t in range(2)]).then_inc(filled, 1)
                elif kind == "y":
                    if n == 0:
                        pe.wait_ge(ld_o, 16)
                    drained(pe, "oT", n)
                    bank, filled = take(kind, n)
                    for t in range(2):
                        mm = product(bank[:, D * t:D * (t + 1)], lambda k: tT[:, 2 * (n % 2) + t, k],
                                     lambda k: wo_sb[:, k])
                    mm.then_inc(filled, 1)
                elif kind == "u2T":
                    pe.wait_ge(u2_ready, n // 2 + 1)
                    bank, filled = take(kind, n)
                    turn(bank, [u2[:, 2 * (n % 2) + t] for t in range(2)]).then_inc(filled, 1)
                elif kind == "ff":
                    if n == 0:
                        drained(pe, "foldB", 0)
                    drained(pe, "u2T", n // 2)
                    bank, filled = take(kind, n)
                    product(bank, lambda k: tT[:, n % UT, k], lambda k: fg[:, k]).then_inc(filled, 1)

        @block.vector
        def _(dve):
            count = [0]

            def mark(ins):
                count[0] += 1
                ins.then_inc(dve_chain, 1)
                return count[0]

            def after(n):
                dve.wait_ge(dve_chain, n)

            def link(ins):
                after(mark(ins))

            def tt(o, a, b, op):
                return dve.tensor_tensor(o, a, b, op)

            def ts(o, a, s1, op1, s2=None, op2=None):
                if op2 is None:
                    return dve.tensor_scalar(o, a, s1, None, op1)
                return dve.tensor_scalar(o, a, s1, s2, op1, op2)

            def stt(o, a, s, b, op1, op2):
                return dve.scalar_tensor_tensor(o, a, s, b, op1, op2)

            dumps = [0, 0]

            def dot(a, b, o):
                if dumps[-2]:
                    after(dumps[-2])
                ins = dve.tensor_tensor_reduce(dump[:, len(dumps) % 2], a, b, 1.0, 0.0, ALU.mult, ALU.add, o)
                dumps.append(mark(ins))
                return dumps[-1]

            def rsqrt(y, a, t):
                link(ts(y.bitcast(I32), a.bitcast(I32), -0.5, ALU.mult, float(0x5F3759DF), ALU.add))
                for _ in range(3):
                    link(tt(t, y, y, ALU.mult))
                    link(stt(t, t, -0.5, a, ALU.mult, ALU.mult))
                    link(stt(y, t, 1.5, y, ALU.add, ALU.mult))

            def atanh(o, n, w):
                om, q, e2, p1, m1, num, den = (t[:, 0:w] for t in rowt[4:11])
                link(ts(om, n, -1.0, ALU.mult, 1.0, ALU.add))
                link(dve.reciprocal(q, om))
                link(stt(q, n, 1.0, q, ALU.add, ALU.mult))
                link(ts(e2.bitcast(I32), q.bitcast(I32), 0x7F800000, ALU.bitwise_and))
                mark(ts(p1, e2, 1.0, ALU.add))
                mark(ts(m1, e2, -1.0, ALU.mult, 1.0, ALU.add))
                link(ts(q.bitcast(I32), e2.bitcast(I32), 23, ALU.logical_shift_right))
                mark(tt(num, n, p1, ALU.mult))
                mark(tt(den, n, m1, ALU.mult))
                link(ts(q, q.bitcast(I32), 127.0, ALU.subtract, math.log(2.0) / 2, ALU.mult))
                mark(tt(num, num, m1, ALU.add))
                link(tt(den, den, p1, ALU.add))
                link(dve.reciprocal(den, den))
                link(tt(num, num, den, ALU.mult))
                link(tt(den, num, num, ALU.mult))
                link(ts(om, den, ATANH[-1], ALU.mult))
                for c in ATANH[-2:0:-1]:
                    link(stt(om, om, c, den, ALU.add, ALU.mult))
                link(stt(om, om, ATANH[0], num, ALU.add, ALU.mult))
                link(tt(o, om, q, ALU.add))

            def row_norms(st, n2, rstd, w):
                t1, t2, n, s = (t[:, 0:w] for t in rowt[0:4])
                mean, var = st[:, :, 0], st[:, :, 1]
                link(tt(t1, mean, mean, ALU.mult))
                link(tt(t1, t1, var, ALU.add))
                mark(ts(n2, t1, float(D), ALU.mult))
                link(ts(t1, t1, float(D), ALU.mult, EPS2, ALU.max))
                rsqrt(t2, t1, n)
                link(tt(n, t1, t2, ALU.mult))
                link(ts(n, n, MAX_TANH, ALU.min))
                atanh(s, n, w)
                link(tt(s, s, t2, ALU.mult))
                link(tt(t1, s, s, ALU.mult))
                link(tt(t1, t1, var, ALU.mult))
                link(ts(t1, t1, 1e-6, ALU.add))
                rsqrt(t2, t1, n)
                link(tt(rstd, s, t2, ALU.mult))

            def row_stats(st, rows, w):
                last = [mark(dve.bn_stats(bn[:, t], rows[:, t])) for t in range(w)]
                for t in range(w):
                    after(last[t])
                    last[t] = mark(dve.bn_aggr(st[:, t], bn[:, t]))
                after(last[-1])

            def clip(r, n2, t):
                link(ts(n2, n2, EPS2, ALU.max))
                rsqrt(r, n2, t)
                link(ts(r, r, A, ALU.mult, 1.0, ALU.min))

            def modulate(o, rows, st, rstd, scale, shift, w, u_sem, each):
                first = []
                for t in range(w + 1):
                    if t < w:
                        first.append(mark(stt(o(t), rows(t), st(t), scale, ALU.subtract, ALU.mult)))
                    if t:
                        after(first[t - 1])
                        row = stt(o(t - 1), o(t - 1), rstd(t - 1), shift, ALU.mult, ALU.add)
                        if each or t == w:
                            row.then_inc(u_sem, 1)
                        else:
                            mark(row)

            def mobius_norm():
                link(ts(s12, s12, EPS2, ALU.max))
                rsqrt(rs12, s12, ts12)
                mark(ts(r_, r_, A, ALU.mult, 1.0, ALU.min))
                link(tt(n_, s2, r_s2, ALU.mult))
                link(tt(n_, n_, r_, ALU.mult))
                ts(tanh_in, n_, EPS, ALU.max).then_inc(norm_ready, 1)

            def mobius_factors(x2, tanhs):
                dve.wait_ge(norm_ready, tanhs)
                mark(ts(b_, x2, -1.0, ALU.mult, 1.0, ALU.add))
                link(dve.reciprocal(n_, tanh_in))
                link(tt(n_, n_, r_, ALU.mult))
                dve.wait_ge(tanh_ready, tanhs)
                link(tt(al, tanh_out, n_, ALU.mult))
                mark(tt(y2, al, al, ALU.mult))
                mark(stt(p_, s3, 2.0, al, ALU.mult, ALU.mult))
                link(tt(b_, b_, al, ALU.mult))
                mark(tt(y2, y2, s2, ALU.mult))
                link(ts(p_, p_, 1.0, ALU.add))
                mark(tt(a_, p_, y2, ALU.add))
                link(tt(t_, x2, y2, ALU.mult))
                link(tt(t_, t_, p_, ALU.add))
                link(ts(t_, t_, EPS, ALU.max))
                link(dve.reciprocal(t_, t_))
                mark(tt(a_, a_, t_, ALU.mult))
                link(tt(b_, b_, t_, ALU.mult))

            dve.wait_ge(ld_bada, 16)
            for part in (SC1, SC2):
                mark(ts(bada_sb[:, D * part:D * (part + 1)], bada_sb[:, D * part:D * (part + 1)], 1.0, ALU.add))
            for i in range(2):
                dve.wait_ge(ld_x[i], 16)
            row_stats(stats[:, 0:TB], x_sb[:, 0:TB], TB)
            row_norms(stats[:, 0:TB], x_n2[:, 0:TB], x_rstd[:, 0:TB], TB)
            tanhs = 0

            for kind, n in TIMELINE:
                if kind == "ada":
                    bank, freed = full(dve, kind, n)
                    tt(mods[:, n // 3, 2 * (n % 3):2 * (n % 3) + 2].rearrange("p m d -> p (m d)"), bank,
                       bada_sb[:, 512 * (n % 3):512 * (n % 3 + 1)], ALU.add).then_inc(freed, 1)
                elif kind == "x_stats":
                    for i in range(2 * n, 2 * n + 2):
                        dve.wait_ge(ld_x[i], 16)
                    row_stats(stats[:, TB * n:TB * (n + 1)], x_sb[:, TB * n:TB * (n + 1)], TB)
                    row_norms(stats[:, TB * n:TB * (n + 1)], x_n2[:, TB * n:TB * (n + 1)],
                              x_rstd[:, TB * n:TB * (n + 1)], TB)
                elif kind in ("u_all", "u"):
                    w, dst = (TB, u_batch) if kind == "u_all" else (CH, u_two)
                    t0 = 0 if kind == "u_all" else CH * n
                    b = t0 // TB
                    if kind == "u_all":
                        for i in range(6):
                            drained(dve, "ada", i)
                    modulate(lambda t: dst[:, t], lambda t: x_sb[:, t0 + t], lambda t: stats[:, t0 + t, 0:1],
                             lambda t: x_rstd[:, t0 + t:t0 + t + 1], mods[:, b, SC1], mods[:, b, SH1], w,
                             u_ready, True)
                    if kind == "u_all":
                        dve.wait_ge(usq_ready, TB)
                        clip(ru, usq, clip_t)
                elif kind == "u_sq":
                    dve.wait_ge(usq_ready, CH * (n + 1))
                    clip(ru[:, 0:CH], usq[:, 0:CH], clip_t[:, 0:CH])
                elif kind == "uT" and CH * n >= TB:
                    bank, freed = full(dve, kind, n)
                    dve.tensor_copy(uT.rearrange("p t k m -> p (t k m)"), bank).then_inc(freed, 1)
                elif kind in ("za", "zb"):
                    if n == 0:
                        dve.wait_ge(ld_bqkv, 16)
                    t0 = CH * n if CH * n < TB else 0
                    t = int(kind == "zb")
                    bank, freed = full(dve, kind, n)
                    if n and not t:
                        after(values)
                    stt(z[:, t, 0:2 * D], bank, ru[:, t0 + t:t0 + t + 1], bqkv_sb[:, 0:2 * D],
                        ALU.mult, ALU.add).then_inc(freed, 1)
                    if kind == "za":
                        bank, freed = full(dve, "zv", n)
                        stt(z[:, 0, 2 * D:], bank[:, 0:D], ru[:, t0:t0 + 1], bqkv_sb[:, 2 * D:],
                            ALU.mult, ALU.add).then_inc(z_ready, 1)
                        stt(z[:, 1, 2 * D:], bank[:, D:2 * D], ru[:, t0 + 1:t0 + 2], bqkv_sb[:, 2 * D:],
                            ALU.mult, ALU.add).then_inc(freed, 1)
                    else:
                        drained(dve, "zb", n)
                        dve.sem_inc(z_ready, 1)
                elif kind == "split":
                    nh = CH * 3 * H
                    for t in range(CH):
                        dve.wait_ge(zsq_ready, CH * n + t + 1)
                        link(dve.tensor_reduce(ss[:, 3 * H * t:3 * H * (t + 1)],
                                               sq[:, t].rearrange("p (h e) -> p h e", e=HD), AX_X, ALU.add))
                    link(dve.tensor_reduce(ss[:, nh:], ss[:, 0:nh].rearrange("p (s h) -> p s h", h=H), AX_X, ALU.add))
                    link(ts(ss, ss, EPS2, ALU.max))
                    rsqrt(rn, ss, split_t)
                    link(ts(rn[:, nh:], rn[:, nh:], C * A, ALU.mult, C, ALU.min))
                    link(stt(ss[:, 0:nh].rearrange("p (s h) -> p s h", h=H),
                             rn[:, 0:nh].rearrange("p (s h) -> p s h", h=H), A,
                             rn[:, nh:].unsqueeze(2).to_broadcast([P, CH * 3, H]), ALU.mult, ALU.min))
                    f = ss[:, 0:nh].rearrange("p (t h) -> p t h", t=CH)
                    qk = [mark(tt(z[:, t, 0:2 * D].rearrange("p (h e) -> p h e", e=HD),
                                  z[:, t, 0:2 * D].rearrange("p (h e) -> p h e", e=HD),
                                  f[:, t, 0:2 * H].unsqueeze(2).to_broadcast([P, 2 * H, HD]), ALU.mult))
                          for t in range(CH)]
                    his = []
                    for t in range(CH):
                        after(qk[t])
                        for s, parts in ((0, q_parts), (1, k_parts)):
                            his.append(mark(dve.tensor_copy(
                                parts[:, H * t:H * (t + 1), 0],
                                z[:, t, D * s:D * (s + 1)].rearrange("p (h e) -> p h e", e=HD))))
                    los = []
                    for t in range(CH):
                        for s, parts, lo in ((0, q_parts, 2), (1, k_parts, 1)):
                            after(his[2 * t + s])
                            los.append(mark(tt(parts[:, H * t:H * (t + 1), lo],
                                               z[:, t, D * s:D * (s + 1)].rearrange("p (h e) -> p h e", e=HD),
                                               parts[:, H * t:H * (t + 1), 0], ALU.subtract)))
                    mark(dve.tensor_copy(q_parts[:, :, 1], q_parts[:, :, 0]))
                    after(los[-1])
                    mark(dve.tensor_copy(q_parts[:, :, 3], q_parts[:, :, 2]))
                    dve.tensor_copy(k_parts[:, :, 2:4], k_parts[:, :, 0:2]).then_inc(parts_ready, 1)
                    for t in range(CH):
                        values = mark(tt(v1[:, CH * n + t, :, 0:HD], z[:, t, 2 * D:3 * D].rearrange("p (h e) -> p h e", e=HD),
                                f[:, t, 2 * H:3 * H].unsqueeze(2).to_broadcast([P, H, HD]), ALU.mult))
                elif kind == "qkT" and n >= TB:
                    for key, dst in (("kT", kT), ("qT", qT)):
                        bank, freed = full(dve, key, n)
                        dve.tensor_copy(dst[:, 1, :, P * (n - TB):P * (n - TB + 1)],
                                        bank.bitcast(F16).rearrange("p (h m) -> p h m", m=P)).then_inc(freed, 1)
                elif kind == "stage":
                    b, _, hg = group(n)
                    if n == 0:
                        dve.wait_ge(consts, 4)
                    if n >= 2:
                        dve.wait_ge(sums_done, KT * (n - 1))
                    for t in range(TB * b, TB * (b + 1)):
                        drained(dve, "kT", t)
                    for odd in range(2):
                        rows = slice(64 * odd, 64 * odd + 64)
                        last = dve.tensor_copy(kz[rows, n % 2, odd::2], kT[rows, b, 2 * hg:2 * hg + 2])
                    last.then_inc(kz_ready, 1)
                elif kind == "sums_zero":
                    for i in range(SUMS, 8):
                        dve.wait_ge(bank_free[i], BANK_USES[i])
                    dve.memset(acc_ps[:], 0.0).then_inc(sums_zeroed, 1)
                elif kind == "acc":
                    dve.wait_ge(sums_done, KT * (n + 1))
                    if n:
                        full(dve, "accT", n - 1)
                    dve.tensor_copy(accT[:], acc_ps[:, n % 2]).then_inc(acc_ready, 1)
                elif kind == "accT":
                    b, qh, hg = group(n)
                    bank, freed = full(dve, kind, n)
                    rows = bank.rearrange("p (t h e) -> p t h e", h=HG, e=32)
                    link(dve.reciprocal(rden, rows[:, :, :, HD]))
                    o = attn[b][:, UT * qh:UT * (qh + 1), HG * HD * hg:HG * HD * (hg + 1)]
                    tt(o.rearrange("p t (h e) -> p t h e", e=HD), rows[:, :, :, 0:HD],
                       rden.unsqueeze(3).to_broadcast([P, UT, HG, HD]), ALU.mult).then_inc(freed, 1)
                elif kind in ("oT", "u2T"):
                    bank, freed = full(dve, kind, n)
                    dve.tensor_copy(tT[:, 2 * (n % 2):2 * (n % 2) + 2].rearrange("p t k m -> p (t k m)"), bank
                                    ).then_inc(freed, 1)
                elif kind == "y":
                    if n == 0:
                        dve.wait_ge(ld_bo, 16)
                    bank, freed = full(dve, kind, n)
                    mark(stt(y_sb[:, 2 * (n % 2)], bank[:, 0:D], 1.0 / C, bo_sb[:], ALU.mult, ALU.add))
                    stt(y_sb[:, 2 * (n % 2) + 1], bank[:, D:], 1.0 / C, bo_sb[:], ALU.mult, ALU.add).then_inc(freed, 1)
                elif kind == "gy":
                    drained(dve, "y", 2 * n + 1)
                    b = UT * n // TB
                    tt(x1, y_sb, mods[:, b, G1].unsqueeze(1).to_broadcast([P, UT, D]), ALU.mult).then_inc(gy_ready, 1)
                    dve.wait_ge(gy_ready, 2 * n + 1)
                    for t in range(UT):
                        last = dot(x1[:, t], x_sb[:, UT * n + t], s3[:, t:t + 1])
                    after(last)
                elif kind == "mid":
                    dve.wait_ge(ysq_ready, 2 * n + 1)
                    mobius_norm()
                elif kind == "mid_tanh":
                    tanhs += 1
                    b = UT * n // TB
                    mobius_factors(x_n2[:, UT * n:UT * (n + 1)], tanhs)
                    xa = [mark(ts(y_sb[:, t], x_sb[:, UT * n + t], a_[:, t:t + 1], ALU.mult)) for t in range(UT)]
                    for t in range(UT):
                        after(xa[t])
                        xa[t] = mark(stt(x1[:, t], x1[:, t], b_[:, t:t + 1], y_sb[:, t], ALU.mult, ALU.add))
                    after(xa[-1])
                    row_stats(st1, x1, UT)
                    row_norms(st1, n2_1, rstd1, UT)
                    if n:
                        dve.wait_ge(stored, 16 * n)
                    modulate(lambda t: u2[:, t], lambda t: x1[:, t], lambda t: st1[:, t, 0:1],
                             lambda t: rstd1[:, t:t + 1], mods[:, b, SC2], mods[:, b, SH2], UT,
                             u2_ready, False)
                    dve.wait_ge(u2_ready, n + 1)
                    for t in range(UT):
                        dot(u2[:, t], fg_row[:, D:2 * D], d2[:, t:t + 1])
                elif kind == "u2_norm":
                    dve.wait_ge(u2sq_ready, n + 1)
                    clip(r2, usq2, t_)
                elif kind == "ff":
                    bank, freed = full(dve, kind, n)
                    t = n % UT
                    mark(dve.tensor_copy(y_sb[:, t], bank[:, 0:D]))
                    after(dumps[-1])
                    dve.tensor_tensor_reduce(dump[:, 0], u2[:, t], bank[:, D:2 * D], 1.0, 0.0, ALU.mult, ALU.add,
                                             d1[:, t:t + 1]).then_inc(freed, 1)
                    drained(dve, kind, n)
                elif kind == "end":
                    b = UT * n // TB
                    mark(tt(d2, d2, r2, ALU.mult))
                    link(tt(t_, r2, r2, ALU.mult))
                    link(tt(d1, d1, t_, ALU.mult))
                    link(stt(d1, d2, 2.0, d1, ALU.mult, ALU.add))
                    if n == 0:
                        dve.wait_ge(b1sq_ready, 1)
                        dve.wait_ge(ld_b2, 16)
                    link(ts(d1, d1, b1_n2, ALU.add))
                    clip(r1, d1, t_)
                    link(tt(r2, r1, r2, ALU.mult))
                    rows = []
                    for t in range(UT):
                        rows.append(mark(stt(gz[:, t], fg_row[:, 0:D], r1[:, t:t + 1], b2_sb[:], ALU.mult, ALU.add)))
                    for t in range(UT):
                        after(rows[t])
                        rows[t] = mark(stt(y_sb[:, t], y_sb[:, t], r2[:, t:t + 1], gz[:, t], ALU.mult, ALU.add))
                    after(rows[-1])
                    tt(gz, y_sb, mods[:, b, G2].unsqueeze(1).to_broadcast([P, UT, D]), ALU.mult).then_inc(gy_ready, 1)
                    dve.wait_ge(gy_ready, 2 * n + 2)
                    for t in range(UT):
                        last = dot(gz[:, t], x1[:, t], s3[:, t:t + 1])
                    after(last)
                elif kind == "end_norm":
                    dve.wait_ge(ysq_ready, 2 * n + 2)
                    mobius_norm()
                elif kind == "end_tanh":
                    tanhs += 1
                    mobius_factors(n2_1, tanhs)
                    xa = [mark(stt(y_sb[:, t], x1[:, t], a_[:, t:t + 1], x_sb[:, UT * n + t], ALU.mult, ALU.add))
                          for t in range(UT)]
                    for t in range(UT):
                        after(xa[t])
                        last = stt(u2[:, t], gz[:, t], b_[:, t:t + 1], y_sb[:, t], ALU.mult, ALU.add)
                        if t < UT - 1:
                            mark(last)
                    last.then_inc(out_ready, 1)




def kernel(x, cond_1024, L0_cond_w_q, L0_cond_b_q, L0_cond_w_k, L0_cond_b_k, L0_cond_w_v, L0_cond_b_v,
           L0_cond_w_o, L0_cond_b_o, L0_cond_w_f1, L0_cond_b_f1, L0_cond_w_f2, L0_cond_b_f2,
           L0_cond_w_ada, L0_cond_b_ada):
    import concourse.bacc as bacc
    from concourse.bass_utils import run_bass_kernel_spmd

    def rows(w):
        w = np.asarray(w)
        return np.ascontiguousarray(w.reshape(-1, P, w.shape[-1]).transpose(1, 0, 2))

    w_qkv = np.concatenate([np.asarray(w) for w in (L0_cond_w_q, L0_cond_w_k, L0_cond_w_v)], axis=1)
    b_qkv = np.concatenate([np.asarray(b) for b in (L0_cond_b_q, L0_cond_b_k, L0_cond_b_v)])
    b1 = np.asarray(L0_cond_b_f1)
    arrays = {
        "in_x": rows(np.asarray(x).reshape(B * S, D)),
        "in_cond_t": rows(np.ascontiguousarray(np.asarray(cond_1024).T)),
        "in_w_ada": rows(L0_cond_w_ada), "in_b_ada": np.asarray(L0_cond_b_ada),
        "in_w_qkv": rows(w_qkv), "in_b_qkv": b_qkv,
        "in_w_o": rows(L0_cond_w_o), "in_b_o": np.asarray(L0_cond_b_o),
        "in_w_f1": rows(L0_cond_w_f1), "in_b_f1": b1,
        "in_b_f1_cols": np.ascontiguousarray(b1.reshape(KF, P).T),
        "in_w_f2": rows(L0_cond_w_f2), "in_b_f2": np.asarray(L0_cond_b_f2),
    }
    nc = bacc.Bacc("TRN2", target_bir_lowering=False, num_devices=1)
    ap = {k: nc.dram_tensor(k, a.shape, mybir.dt.from_np(a.dtype), kind="ExternalInput").ap()
          for k, a in arrays.items()}
    out = nc.dram_tensor("out_x", (P, TILES, D), F32, kind="ExternalOutput").ap()
    build(nc, ap["in_x"], ap["in_cond_t"], ap["in_w_ada"], ap["in_b_ada"], ap["in_w_qkv"], ap["in_b_qkv"],
          ap["in_w_o"], ap["in_b_o"], ap["in_w_f1"], ap["in_b_f1"], ap["in_b_f1_cols"], ap["in_w_f2"],
          ap["in_b_f2"], out)
    got = run_bass_kernel_spmd(nc, [arrays], core_ids=[0]).results[0]["out_x"]
    return got.transpose(1, 0, 2).reshape(B, S, D)
```

```python
import math
from contextlib import ExitStack

import numpy as np

import concourse.bass as bass
from concourse import mybir

F32 = mybir.dt.float32
F16 = mybir.dt.float16
I32 = mybir.dt.int32
ALU = mybir.AluOpType
ACT = mybir.ActivationFunctionType
AX_X = mybir.AxisListType.X

P = 128
B, S, D, H, FF = 2, 1024, 256, 16, 1024
HD = D // H
KD = D // P
KF = FF // P
TILES = B * S // P
TB = TILES // B
CH = 2
HG = 4
RING = 3
QW = 512
GROUPS = B * (S // QW) * (H // HG)
KT = S // P
KTU = 2
UNITS = GROUPS * KT * KTU
SUMS_LAG = 2
UT = QW // P
LAYER_UNITS = TILES // UT
LAST_ROWS = UT * (LAYER_UNITS - 1)

EPS = 1e-7
EPS2 = EPS * EPS
MAX_TANH = float(np.float32(1.0 - 1e-5))
A = math.atanh(MAX_TANH)


def _beta(a, b):
    return math.exp(math.lgamma(a) + math.lgamma(b) - math.lgamma(a + b))


C = _beta(HD / 2, 0.5) / _beta(D / 2, 0.5)
assert C * C > H and A * A / math.sqrt(HD) < 60

SH1, SC1, G1, SH2, SC2, G2 = range(6)


def _atanh_series():
    w = (0.5 - 0.5 * np.cos(np.pi * (np.arange(2000) + 0.5) / 2000)) * 9 / 49
    fit = np.polynomial.chebyshev.Chebyshev.fit(w, np.arctanh(np.sqrt(w)) / np.sqrt(w), 4)
    return [float(c) for c in fit.convert(kind=np.polynomial.Polynomial).coef]


ATANH = _atanh_series()


def group(g):
    n = H // HG
    return g // (2 * n), g // n % 2, g % n


def key_tile_order():
    first = [(g, kt) for part in (range(0, 4), range(4, 6), range(6, KT)) for g in range(2) for kt in part]
    return first + [(g, kt) for g in range(2, GROUPS) for kt in range(KT)]


ORDER = key_tile_order()
LAST = [ORDER.index((g, KT - 1)) for g in range(GROUPS)]
STAGES = [(g, *part) for part in ((0, 4), (4, 6), (6, KT)) for g in range(2)] + \
    [(g, 0, KT) for g in range(2, GROUPS)]


def timeline():
    fill = {}

    def put(unit, *jobs):
        for job in jobs:
            fill.setdefault(int(unit), []).append(job)

    out = [("ada", 0), ("ada_add", 0)] + [("ada", i) for i in range(1, 5)] + [("x_rstd", 0), ("u_first", 0)]
    out += [("uT", 0), ("u_rest", 0), ("za", 0), ("zv", 0), ("zb", 0), ("ada_add", 1), ("ada_add", 2), ("split", 0)]
    out += [("foldT", i) for i in range(4)] + [("ada", 5), ("ada_add", 3), ("ada_add", 4), ("uT", 1), ("ada_add", 5)]
    out += [("parts", 0), ("za", 1), ("zv", 1), ("zb", 1), ("split", 1), ("qkT", 0), ("qkT", 1)]
    out += [("foldF", 0), ("uT", 2), ("parts", 1), ("za", 2), ("zv", 2), ("zb", 2), ("uT", 3), ("split", 2)]
    out += [("qkT", 2), ("qkT", 3), ("foldP", 0), ("foldF", 1), ("parts", 2), ("za", 3), ("zv", 3)]
    out += [("qkT", 4), ("qkT", 5), ("zb", 3), ("foldB", 0), ("sums_zero", 0), ("split", 3)]
    out += [("stage", 0), ("stage", 1), ("stage", 2), ("stage", 3)]

    for n, job in EARLY:
        put(n, job)

    for c, n in zip(range(TB // CH, TILES // CH), PROJ_AT):
        for kind, later in PROJ_STEPS:
            put(n + later, (kind, c))
        put(n + QKT_STEPS[0], ("qkT", 2 * c))
        put(n + QKT_STEPS[1], ("qkT", 2 * c + 1))

    def layers(v, n, d):
        for kind, each, later in LAYER_STEPS:
            for i, m in enumerate(later):
                put(n + m * d, (kind, each * v + i))

    for v, n in enumerate(LAYERS_AT):
        layers(v, n, LAYERS_PACE[v])

    for n in range(UNITS):
        out.append(("exp", n))
        if n % KTU == 0 and n >= SUMS_LAG * KTU:
            out.append(("sums", n // KTU - SUMS_LAG))
        for g in range(GROUPS):
            if n == KTU * LAST[g] + ACC_STEPS[0]:
                out.append(("acc", g))
            if n == KTU * LAST[g] + ACC_STEPS[1]:
                out.append(("accT", g))
            if g >= 2 and n == KTU * LAST[g - 2] + 4:
                out.append(("stage", STAGES.index((g, 0, KT))))
        out += fill.pop(n, [])
    out += [("sums", UNITS // KTU - i) for i in range(SUMS_LAG, 0, -1)]
    last = {kind: [(kind, each * (LAYER_UNITS - 1) + i) for i in range(each)] for kind, each, _ in LAYER_STEPS}
    out += [("acc", GROUPS - 1), ("accT", GROUPS - 1)] + last.pop("oT")
    for n in sorted(fill):
        out += fill[n]
    for jobs in last.values():
        out += jobs
    return out


EARLY = (
    (0, ("parts", 3)), (13, ("qkT", 6)), (13, ("qkT", 7)), (12, ("stage", 4)), (14, ("stage", 5)),
    (2, ("x_stats", 1)), (9, ("x_norm", 1)), (22, ("x_rstd", 1)))
PROJ_AT = (22, 46, 76, 100)
PROJ_STEPS = (
    ("u", 0), ("u_sq", 2), ("uT", 2), ("za", 5), ("zv", 5), ("zb", 7), ("split", 7), ("parts", 12))
QKT_STEPS = (21, 23)
LAYERS_AT = (72, 138, 201)
LAYERS_PACE = (1.0, 1.0, 0.9)
LAYER_STEPS = (
    ("oT", 2, (0, 0)), ("y", 2, (3, 3)), ("gy", 1, (6,)), ("mid_sq", 4, (7, 8, 10, 10)), ("mid", 1, (10,)),
    ("mid_tanh", 1, (14,)), ("x1", 1, (17,)), ("x1_norm", 1, (21,)), ("x1_rstd", 1, (25,)), ("u2", 1, (29,)),
    ("u2_sq", 4, (32, 33, 34, 35)), ("u2T", 2, (32, 32)), ("u2_norm", 1, (36,)), ("ffG", 2, (35, 37)),
    ("ffF", 2, (41, 43)), ("end", 1, (39,)), ("end_y", 1, (43,)), ("end_sq", 4, (49, 50, 51, 52)),
    ("end_norm", 1, (52,)), ("end_tanh", 1, (56,)))
ACC_STEPS = (6, 9)
ON_POOL = 1
TIMELINE = timeline()

SCORES, SUMS = 2, 6


BANKS = {
    "ada": lambda n: {0: SUMS, 5: SUMS + 1}.get(n, SCORES + n - 1),
    "foldT": lambda n: SUMS + n % 2, "foldF": lambda n: SUMS + n, "foldP": lambda n: SUMS, "foldB": lambda n: SUMS,
    "uT": lambda n: 0, "za": lambda n: 1, "zv": lambda n: 0, "zb": lambda n: SUMS + 1 if n < 4 else 1,
    "qT": lambda n: SCORES + 2 * (n % 2) if n < 6 else 0, "kT": lambda n: SCORES + 1 + 2 * (n % 2) if n < 6 else 1,
    "accT": lambda n: n % 2, "oT": lambda n: n % 2, "y": lambda n: n % 2, "u2T": lambda n: n % 2,
    "ffG": lambda n: n % 2, "ffF": lambda n: n % 2,
}

EARLY_TILES = {"u_first": range(0, CH), "u_rest": range(CH, TB)}

TOKEN_STEPS = ("x_rstd", "u_first", "u_rest", "u_sq", "x1_rstd", "mid", "mid_tanh", "u2_norm", "end", "end_norm",
               "end_tanh")


def uses_of_banks():
    at, count = {}, [0] * 8
    for kind, n in TIMELINE:
        for key in ("kT", "qT") if kind == "qkT" else (kind,):
            if key in BANKS:
                bank = BANKS[key](n)
                at[key, n] = (bank, count[bank])
                count[bank] += 1
    return at, count


BANK_USE, BANK_USES = uses_of_banks()




def build(nc, x, cond_t, w_ada, b_ada, w_qkv, b_qkv, w_o, b_o, w_f1, b_f1, b_f1_cols, w_f2, b_f2, out):
    with ExitStack() as ctx:
        def sb(name, shape, dt=F32):
            return ctx.enter_context(nc.sbuf_tensor(name, shape, dt))

        def sem(name):
            return ctx.enter_context(nc.semaphore(name))

        x_sb = sb("x_sb", [P, TILES, D])
        qT = sb("qT", [P, B, H // 2, S], F16)
        kT = sb("kT", [P, B, H // 2, S], F16)
        kz = sb("kz", [P, 2, HG, S], F16)
        v1 = sb("v1", [P, TILES, H, HD + 1])
        probs = sb("probs", [P, RING, HG, QW])
        attn0 = sb("attn0", [P, TB, D])
        accT = sb("accT", [P, QW])
        wo_sb = sb("wo_sb", [P, KD, D])
        fg = sb("fg", [P, KD, 2 * D])
        fg_row = sb("fg_row", [P, 2 * D])
        wqkv_sb = sb("wqkv_sb", [P, KD, 3 * D])
        bqkv_sb = sb("bqkv_sb", [P, 3 * D])
        bo_sb = sb("bo_sb", [P, D])
        b2_sb = sb("b2_sb", [P, D])
        mods = sb("mods", [P, B, 6, D])
        identf = sb("identf", [P, P])
        ident = sb("ident", [P, P], F16)
        proj = sb("proj", [P, 4608])
        lay = sb("lay", [P, 2, UT, D])
        small = sb("small", [P, 698])

        u_two = proj[:, 0:512].rearrange("p (t d) -> p t d", t=CH)
        uT = proj[:, 512:1024].rearrange("p (t k m) -> p t k m", t=CH, k=KD)
        z = proj[:, 1024:2560].rearrange("p (t n) -> p t n", t=CH)
        sq = proj[:, 2560:4096].rearrange("p (t n) -> p t n", t=CH)
        q_parts = proj[:, 2560:3584].bitcast(F16).rearrange("p (h s e) -> p h s e", s=4, e=HD)
        k_parts = proj[:, 3584:4608].bitcast(F16).rearrange("p (h s e) -> p h s e", s=4, e=HD)
        q_used = qT[:].bitcast(F32)[:, 0, :, 0:D]
        sq_early = lay[:].rearrange("p i t d -> p (i t d)")[:, 0:CH * 3 * D].rearrange("p (t n) -> p t n", t=CH)
        sqs = [sq_early if c < TB // CH else sq for c in range(TILES // CH)]
        y_sb, x1 = q_used[:, 0:UT], q_used[:, UT:2 * UT]
        u2 = lay[:, 0]
        v_used = v1[:, 0:TB].rearrange("p t h e -> p (t h e)")[:, 0:UT * D]
        tTs = [lay[:, 1].rearrange("p t (k m) -> p t k m", k=KD)] + \
            [v_used.rearrange("p (t k m) -> p t k m", t=UT, k=KD)] * (LAYER_UNITS - 1)
        gz = lay[:, 1]
        pr = probs[:].rearrange("p r h q -> p (r h q)")
        w2w1 = pr[:, 0:4096].rearrange("p (f n) -> p f n", f=KF)
        b1_sb = pr[:, 4096:4096 + FF]
        ada_sb = qT[:, 1].rearrange("p h s -> p (h s)").bitcast(F32)[:, 0:3072].rearrange("p (k n) -> p k n", k=KD)
        k_later = kT[:, 1].rearrange("p h s -> p (h s)").bitcast(F32)
        u_batch = k_later[:, 0:TB * D].rearrange("p (t d) -> p t d", d=D)
        bada_sb = k_later[:, TB * D:TB * D + 6 * D]
        w1_sb = attn0[:].rearrange("p t d -> p (t d)").rearrange("p (k n) -> p k n", k=KD)
        attn1 = kT[:, 0].rearrange("p h s -> p (h s)").bitcast(F32)[:, 0:TB * D].rearrange("p (t d) -> p t d", d=D)
        attn = [attn0[:], attn1]

        dump = mods[:, 0, SH1:SC1 + 1]

        def u_of(c):
            return u_batch[:, CH * c:CH * (c + 1)] if CH * c < TB else u_two

        at = [0]

        def cols(n):
            at[0] += n
            return small[:, at[0] - n:at[0]]

        stats = cols(2 * TILES).rearrange("p (t s) -> p t s", s=2)
        x_n2, x_rstd, b1_n2 = cols(TILES), cols(TILES), cols(1)
        cols(1)
        cond_sb = cols(KD * B).rearrange("p (k b) -> p k b", k=KD)
        b1c_sb, part_sum = cols(KF), cols(1)
        cols(1)
        b1_parts = attn0[:].rearrange("p t d -> p (t d)")[:, 0:2 * D]
        bn = cols(6 * TB).rearrange("p (t s) -> p t s", s=6)
        rowt = [cols(TB) for _ in range(10)]
        usq, ru, clip_t = cols(TB), cols(TB), cols(TB)
        W3 = CH * 3 * (H + 1)
        ss, rn, split_t = cols(W3), cols(W3), cols(W3)
        rden = cols(UT * HG).rearrange("p (t h) -> p t h", h=HG)
        s12, rs12, ts12 = cols(2 * UT), cols(2 * UT), cols(2 * UT)
        s1, s2, r_, r_s2 = s12[:, 0:UT], s12[:, UT:], rs12[:, 0:UT], rs12[:, UT:]
        s3, n_, al, y2, p_, a_, b_, t_, n2_1, rstd1, r2, usq2, d1, d2, r1 = (cols(UT) for _ in range(15))
        pool_spare, r22 = cols(TB), cols(UT)
        tanh_in, tanh_out, clip2_t = cols(UT), cols(UT), cols(UT)
        st1 = cols(2 * UT).rearrange("p (t s) -> p t s", s=2)

        wk_ps = ctx.enter_context(nc.psum_tensor("wk_ps", [P, 2, 512], F32))
        sc_ps = ctx.enter_context(nc.psum_tensor("sc_ps", [P, 2, 2, QW], F32))
        acc_ps = ctx.enter_context(nc.psum_tensor("acc_ps", [P, 2, QW], F32))
        banks = [wk_ps[:, 0], wk_ps[:, 1], sc_ps[:, 0, 0], sc_ps[:, 0, 1], sc_ps[:, 1, 0], sc_ps[:, 1, 1],
                 acc_ps[:, 0], acc_ps[:, 1]]

        ld_x = [sem(f"ld_x{i}") for i in range(4)]
        ld_cond, ld_bada = sem("ld_cond"), sem("ld_bada")
        ld_ada = [sem(f"ld_ada{i}") for i in range(3)]
        ld_qkv, ld_bqkv, ld_o, ld_bo = sem("ld_qkv"), sem("ld_bqkv"), sem("ld_o"), sem("ld_bo")
        ld_f1, ld_f2, ld_b1, ld_b1c, ld_b2 = sem("ld_f1"), sem("ld_f2"), sem("ld_b1"), sem("ld_b1c"), sem("ld_b2")
        consts = sem("consts")
        bank_full = [sem(f"bank{i}_full") for i in range(8)]
        bank_free = [sem(f"bank{i}_free") for i in range(8)]
        u_ready = sem("u_ready")
        usq_ready = sem("usq_ready")
        zsq_ready = sem("zsq_ready")
        parts_ready = sem("parts_ready")
        kz_ready = [sem(f"kz{i}_ready") for i in range(6)]
        values_ready = sem("values_ready")
        sums_zeroed = sem("sums_zeroed")
        scores_ready = sem("scores_ready")
        probs_ready = sem("probs_ready")
        sums_done = sem("sums_done")
        acc_ready = sem("acc_ready")
        gy_ready = sem("gy_ready")
        y_ready = sem("y_ready")
        ysq_ready = sem("ysq_ready")
        u2_ready, u2sq_ready = sem("u2_ready"), sem("u2sq_ready")
        norm_ready, tanh_ready = sem("norm_ready"), sem("tanh_ready")
        out_ready, stored = sem("out_ready"), sem("stored")
        b1sq_ready = sem("b1sq_ready")
        logs_ready = sem("logs_ready")
        x_stats_ready = sem("x_stats_ready")
        stats_ready = sem("stats_ready")
        centred_ready = sem("centred_ready")
        rstd_ready = sem("rstd_ready")
        ru_ready = sem("ru_ready")
        heads_ready = sem("heads_ready")
        dots_ready = sem("dots_ready")
        ab_ready = sem("ab_ready")
        a_ready = sem("a_ready")
        ax_ready = sem("ax_ready")
        r1_ready = sem("r1_ready")
        dve_chain, pool_chain, act_chain = sem("dve_chain"), sem("pool_chain"), sem("act_chain")

        block = ctx.enter_context(nc.Block())

        def full(eng, key, n):
            bank, use = BANK_USE[key, n]
            eng.wait_ge(bank_full[bank], use + 1)
            return banks[bank], bank_free[bank]

        def drained(eng, key, n):
            bank, use = BANK_USE[key, n]
            eng.wait_ge(bank_free[bank], use + 1)

        def kz_sem(stage):
            return kz_ready[stage if stage < 6 else STAGES[stage][0] % 2]

        def on_pool(kind, n):
            if kind in ("x_rstd", "u_first", "u_rest", "u_sq"):
                return (kind, n) != ("x_rstd", 0)
            return kind in TOKEN_STEPS and n < ON_POOL

        def token_step(work, kind, n):
            eng, mark, link, ts, mul, add = work.eng, work.mark, work.link, work.ts, work.mul, work.add

            def mobius_norm():
                link(ts(s12, s12, EPS2, ALU.max))
                work.rsqrt(rs12, s12, ts12)
                mark(ts(r_, r_, A, ALU.mult, 1.0, ALU.min))
                link(mul(n_, s2, r_s2))
                mul(tanh_in, n_, r_).then_inc(norm_ready, 1)

            def mobius_factors(x2, tanhs):
                mark(ts(b_, x2, -1.0, ALU.mult, 1.0, ALU.add))
                mark(ts(p_, s3, 2.0, ALU.mult))
                eng.wait_ge(tanh_ready, tanhs)
                link(mul(al, tanh_out, r_s2))
                mark(mul(y2, al, al))
                mark(mul(p_, p_, al))
                link(mul(b_, b_, al))
                mark(mul(y2, y2, s2))
                link(ts(p_, p_, 1.0, ALU.add))
                mark(add(a_, p_, y2))
                link(mul(t_, x2, y2))
                link(add(t_, t_, p_))
                ts(t_, t_, EPS, ALU.max).then_inc(ab_ready, 1)

            if kind in ("x_rstd", "x1_rstd"):
                eng.wait_ge(logs_ready, n + 1 if kind == "x_rstd" else B + n + 1)
                st, rstd = ((stats[:, TB * n:TB * (n + 1)], x_rstd[:, TB * n:TB * (n + 1)]) if kind == "x_rstd"
                            else (st1, rstd1))
                w = st.shape[1]
                t2, s = rowt[1][:, 0:w], rowt[3][:, 0:w]
                t1, t0 = rowt[0][:, 0:w], rowt[2][:, 0:w]
                link(mul(s, s, t2))
                link(mul(t1, s, s))
                link(mul(t1, t1, st[:, :, 1]))
                link(ts(t1, t1, 1e-6, ALU.add))
                work.rsqrt(t2, t1, t0)
                mul(rstd, s, t2).then_inc(rstd_ready, 1)
            elif kind in ("u_first", "u_rest"):
                tiles = slice(EARLY_TILES[kind].start, EARLY_TILES[kind].stop)
                eng.wait_ge(usq_ready, tiles.stop)
                work.clip(ru[:, tiles], usq[:, tiles], clip_t[:, tiles]).then_inc(ru_ready, 1)
            elif kind == "u_sq":
                eng.wait_ge(usq_ready, CH * (n + 1))
                drained(eng, "zb", n - 1)
                work.clip(ru[:, 0:CH], usq[:, 0:CH], clip_t[:, 0:CH]).then_inc(ru_ready, 1)
            elif kind == "mid":
                eng.wait_ge(ysq_ready, UT * (2 * n + 1))
                mobius_norm()
            elif kind == "mid_tanh":
                eng.wait_ge(dots_ready, 3 * n + 1)
                mobius_factors(x_n2[:, UT * n:UT * (n + 1)], 2 * n + 1)
            elif kind == "u2_norm":
                eng.wait_ge(u2sq_ready, UT * (n + 1))
                if n == 0:
                    eng.wait_ge(b1sq_ready, 1)
                link(work.clip(r2, usq2, clip2_t))
                eng.wait_ge(dots_ready, 3 * n + 2)
                mark(mul(d2, d2, r2))
                link(mul(r22, r2, r2))
                link(ts(d2, d2, 2.0, ALU.mult, b1_n2, ALU.add))
            elif kind == "end":
                drained(eng, "ffG", 2 * n + 1)
                link(mul(d1, d1, r22))
                link(add(d1, d1, d2))
                link(work.clip(r1, d1, clip2_t))
                mul(r2, r1, r2).then_inc(r1_ready, 1)
            elif kind == "end_norm":
                eng.wait_ge(ysq_ready, UT * (2 * n + 2))
                mobius_norm()
            elif kind == "end_tanh":
                eng.wait_ge(dots_ready, 3 * n + 3)
                mobius_factors(n2_1, 2 * n + 2)

        @block.sync
        def _(sp):
            sp.dma_start(x_sb[:, 0:4], x[:, 0:4]).then_inc(ld_x[0], 16)
            sp.dma_start(cond_sb, cond_t).then_inc(ld_cond, 16)
            for i in range(3):
                sp.dma_start(ada_sb[:, :, 512 * i:512 * (i + 1)], w_ada[:, :, 512 * i:512 * (i + 1)]
                             ).then_inc(ld_ada[i], 16)
            sp.dma_start(wqkv_sb[:], w_qkv).then_inc(ld_qkv, 16)
            sp.dma_start(w1_sb, w_f1).then_inc(ld_f1, 16)
            sp.dma_start(w2w1[:, :, 0:D], w_f2).then_inc(ld_f2, 16)
            for i in range(2, 4):
                sp.dma_start(x_sb[:, 4 * i:4 * i + 4], x[:, 4 * i:4 * i + 4]).then_inc(ld_x[i], 16)
            sp.dma_start(wo_sb[:], w_o).then_inc(ld_o, 16)
            for kind, n in TIMELINE:
                if kind == "stage":
                    g, t0, t1 = STAGES[n]
                    b, _, hg = group(g)
                    if n == 0:
                        sp.wait_ge(consts, 5)
                    if g >= 2:
                        sp.wait_ge(scores_ready, KTU * (LAST[g - 2] + 1))
                    for t in range(t0, t1):
                        drained(sp, "kT", TB * b + t)
                    for odd in range(2):
                        rows = slice(64 * odd, 64 * odd + 64)
                        sp.dma_start(kz[rows, g % 2, odd::2, P * t0:P * t1],
                                     kT[rows, b, 2 * hg:2 * hg + 2, P * t0:P * t1]).then_inc(kz_sem(n), 16)
                elif kind == "end_tanh":
                    sp.wait_ge(out_ready, n + 1)
                    sp.dma_start(out[:, UT * n:UT * (n + 1)], u2).then_inc(stored, 16)
            sp.wait_ge(stored, 16 * LAYER_UNITS)

        @block.gpsimd
        def _(pool):
            n = 0
            for t in (identf, ident):
                pool.memset(t[:], 0.0).then_inc(pool_chain, 1)
                n += 1
                pool.wait_ge(pool_chain, n)
                pool.affine_select(out=t[:], in_=t[:], compare_op=ALU.not_equal, fill=1.0, base=0,
                                   pattern=[[-1, P]], channel_multiplier=1).then_inc(consts, 1)
            pool.memset(v1[:, :, :, HD:HD + 1], 1.0).then_inc(consts, 1)
            pool.memset(part_sum, 1.0 / 32).then_inc(consts, 1)
            pool.memset(kz[:].bitcast(F32), 0.0).then_inc(consts, 1)

            work = Work(pool, pool_chain, spare=pool_spare)
            work.count = n
            for kind, n in TIMELINE:
                if on_pool(kind, n):
                    token_step(work, kind, n)
                elif kind == "x1_norm":
                    pool.wait_ge(stats_ready, n + 1)
                    if n:
                        pool.wait_ge(stored, 16 * n)
                    less_mean = [work.mark(work.ts(u2[:, t], x1[:, t], st1[:, t, 0:1], ALU.subtract))
                                 for t in range(UT)]
                    for t in range(UT):
                        work.after(less_mean[t])
                        work.mul(u2[:, t], u2[:, t], mods[:, UT * n // TB, SC2]).then_inc(centred_ready, 1)
                elif kind == "parts":
                    pool.wait_ge(heads_ready, n + 1)
                    f = ss[:, 0:CH * 3 * H].rearrange("p (t h) -> p t h", t=CH)
                    values = [work.tt(v1[:, CH * n + t, :, 0:HD],
                                      z[:, t, 2 * D:3 * D].rearrange("p (h e) -> p h e", e=HD),
                                      f[:, t, 2 * H:3 * H].unsqueeze(2).to_broadcast([P, H, HD]), ALU.mult)
                              for t in range(CH)]
                    work.mark(values[0])
                    values[1].then_inc(values_ready, 1)

        @block.scalar
        def _(act):
            act.dma_start(x_sb[:, 4:8], x[:, 4:8]).then_inc(ld_x[1], 16)
            act.dma_start(bada_sb, b_ada.partition_broadcast(P)).then_inc(ld_bada, 16)
            act.dma_start(bqkv_sb[:], b_qkv.partition_broadcast(P)).then_inc(ld_bqkv, 16)
            act.dma_start(b1c_sb, b_f1_cols).then_inc(ld_b1c, 16)
            act.dma_start(b1_sb, b_f1.partition_broadcast(P)).then_inc(ld_b1, 16)
            act.dma_start(bo_sb[:], b_o.partition_broadcast(P)).then_inc(ld_bo, 16)
            act.dma_start(b2_sb[:], b_f2.partition_broadcast(P)).then_inc(ld_b2, 16)

            def square(a, junk, total):
                return act.activation(junk, a, ACT.Square, accum_out=total)

            def copy(o, key, n):
                bank, freed = full(act, key, n)
                if o.dtype == F16:
                    bank = bank.bitcast(F16)
                if len(o.shape) == 3:
                    bank = bank.rearrange("p (h m) -> p h m", m=o.shape[2])
                act.activation(o, bank, ACT.Copy).then_inc(freed, 1)

            tanhs = 0
            for kind, n in TIMELINE:
                if kind in ("u_first", "u_rest"):
                    for t in EARLY_TILES[kind]:
                        act.wait_ge(u_ready, t + 1)
                        square(u_batch[:, t], lay[:, t // UT, t % UT], usq[:, t:t + 1]).then_inc(usq_ready, 1)
                elif kind == "u_sq":
                    act.wait_ge(u_ready, CH * (n + 1))
                    for t in range(CH):
                        square(u_two[:, t], sq[:, 0, D * t:D * (t + 1)], usq[:, t:t + 1]).then_inc(usq_ready, 1)
                elif kind == "uT" and CH * n < TB:
                    copy(uT.rearrange("p t k m -> p (t k m)"), kind, n)
                elif kind == "foldT":
                    copy(w2w1[:, 2 * n:2 * n + 2, D:2 * D], kind, n)
                elif kind == "foldF":
                    copy(fg[:, n], kind, n)
                elif kind == "foldP":
                    copy(b1_parts, kind, n)
                    act.wait_ge(ld_b1, 16)
                    square(b1_sb, b1_sb, b1_n2).then_inc(b1sq_ready, 1)
                elif kind == "foldB":
                    copy(fg_row[:], kind, n)
                elif kind == "split":
                    if n == 0:
                        act.wait_ge(usq_ready, TB)
                    if sqs[n] is sq:
                        full(act, "qT", CH * n - 1)
                    for t in range(CH):
                        drained(act, ("zv", "zb")[t], n)
                        act.activation(sqs[n][:, t], z[:, t], ACT.Square).then_inc(zsq_ready, 1)
                elif kind == "qkT" and n < TB:
                    copy(kT[:, 0, :, P * n:P * (n + 1)], "kT", n)
                    copy(qT[:, 0, :, P * n:P * (n + 1)], "qT", n)
                elif kind == "exp":
                    kt = n // KTU
                    act.wait_ge(scores_ready, n + 1)
                    if n % KTU == 0 and kt >= RING:
                        act.wait_ge(sums_done, kt - RING + 1)
                    act.activation(probs[:, kt % RING, 2 * (n % 2):2 * (n % 2) + 2], sc_ps[:, n % 2],
                                   ACT.Exp, scale=1.0 / math.sqrt(HD)).then_inc(probs_ready, 1)
                elif kind == "mid_sq" and n == LAST_ROWS:
                    v = n // UT
                    for t in range(UT):
                        drained(act, "y", 2 * v + t // 2)
                        square(y_sb[:, t], gz[:, t], s1[:, t:t + 1])
                    act.wait_ge(gy_ready, 2 * v + 1)
                    act.wait_ge(stored, 16 * v)
                    for t in range(UT):
                        square(x1[:, t], u2[:, t], s2[:, t:t + 1]).then_inc(ysq_ready, 1)
                elif kind == "acc":
                    act.wait_ge(sums_done, LAST[n] + 1)
                    if n:
                        full(act, "accT", n - 1)
                    act.activation(accT[:], acc_ps[:, n % 2], ACT.Copy).then_inc(acc_ready, 1)
                elif kind == "x1" and n == LAYER_UNITS - 1:
                    act.wait_ge(a_ready, 2 * n + 1)
                    for t in range(UT):
                        act.activation(y_sb[:, t], x_sb[:, UT * n + t], ACT.Copy, scale=a_[:, t:t + 1]
                                       ).then_inc(ax_ready, 1)
                elif kind == "u2_sq" and n == LAST_ROWS:
                    act.wait_ge(u2_ready, n // UT + 1)
                    for t in range(UT):
                        square(u2[:, t], y_sb[:, t], usq2[:, t:t + 1]).then_inc(u2sq_ready, 1)
                elif kind == "end_sq" and n == LAST_ROWS:
                    for t in range(UT):
                        act.wait_ge(y_ready, t + 1)
                        square(y_sb[:, t], u2[:, t], s1[:, t:t + 1]).then_inc(act_chain, 1)
                    act.wait_ge(gy_ready, 2 * (n // UT) + 2)
                    for t in range(UT):
                        act.wait_ge(act_chain, t + 1)
                        square(gz[:, t], u2[:, t], s2[:, t:t + 1]).then_inc(ysq_ready, 1)
                elif kind in ("mid_tanh", "end_tanh"):
                    tanhs += 1
                    act.wait_ge(norm_ready, tanhs)
                    act.activation(tanh_out, tanh_in, ACT.Tanh).then_inc(tanh_ready, 1)

        @block.tensor
        def _(pe):
            def take(key, n):
                bank, use = BANK_USE[key, n]
                if use:
                    pe.wait_ge(bank_free[bank], use)
                return banks[bank], bank_full[bank]

            def product(o, lhs, rhs):
                for k in range(KD):
                    mm = pe.matmul(o, lhs(k), rhs(k), start=(k == 0), stop=(k == KD - 1))
                return mm

            def turn(bank, tiles):
                i = 0
                for tile in tiles:
                    for k in range(KD):
                        mm = pe.transpose(bank[:, P * i:P * (i + 1)], tile[:, P * k:P * (k + 1)], identf[:])
                        i += 1
                return mm

            for kind, n in TIMELINE:
                if kind == "ada":
                    if n == 0:
                        pe.wait_ge(ld_cond, 16)
                    if n < 3:
                        pe.wait_ge(ld_ada[n], 16)
                    bank, filled = take(kind, n)
                    product(bank, lambda k: cond_sb[:, k, n // 3:n // 3 + 1].to_broadcast([P, P]),
                            lambda k: ada_sb[:, k, 512 * (n % 3):512 * (n % 3 + 1)]).then_inc(filled, 1)
                elif kind == "foldT":
                    if n == 0:
                        pe.wait_ge(ld_f1, 16)
                    bank, filled = take(kind, n)
                    for f in range(2 * n, 2 * n + 2):
                        for k in range(KD):
                            i = 2 * (f % 2) + k
                            mm = pe.transpose(bank[:, P * i:P * (i + 1)], w1_sb[:, k, P * f:P * (f + 1)], identf[:])
                    mm.then_inc(filled, 1)
                elif kind == "foldF":
                    bank, filled = take(kind, n)
                    if n == 0:
                        pe.wait_ge(ld_f2, 16)
                    for part in (slice(0, 2 * D),) if n == 0 else (slice(0, D), slice(D + P, 2 * D)):
                        for f in range(KF):
                            mm = pe.matmul(bank[:, part], w2w1[:, f, D + P * n:D + P * (n + 1)], w2w1[:, f, part],
                                           start=(f == 0), stop=(f == KF - 1))
                    if n:
                        drained(pe, "foldF", 0)
                        mm = pe.transpose(bank[:, D:D + P], fg[:, 0, D + P:2 * D], identf[:])
                    mm.then_inc(filled, 1)
                elif kind == "foldP":
                    bank, filled = take(kind, n)
                    pe.wait_ge(ld_b1c, 16)
                    for f in range(KF):
                        j = f % 4
                        mm = pe.matmul(bank[32 * j:32 * (j + 1)], b1c_sb[:, f:f + 1].to_broadcast([P, 32]), w2w1[:, f],
                                       start=(f < 4), stop=(f >= 4), tile_position=(0, 32 * j))
                    mm.then_inc(filled, 1)
                elif kind == "foldB":
                    drained(pe, "foldP", n)
                    bank, filled = take(kind, n)
                    pe.matmul(bank, part_sum.to_broadcast([P, P]), b1_parts, start=True, stop=True
                              ).then_inc(filled, 1)
                elif kind == "uT":
                    bank, filled = take(kind, n)
                    pe.wait_ge(u_ready, CH * (n + 1))
                    if n == 0:
                        pe.wait_ge(consts, 5)
                    turn(bank, [u_of(n)[:, t] for t in range(CH)]).then_inc(filled, 1)
                elif kind == "za":
                    if n == 0:
                        pe.wait_ge(ld_qkv, 16)
                    drained(pe, "uT", n)
                    bank, filled = take("za", n)
                    product(bank, lambda k: uT[:, 0, k], lambda k: wqkv_sb[:, k, 0:2 * D]).then_inc(filled, 1)
                elif kind == "zv":
                    bank, filled = take("zv", n)
                    for t in range(CH):
                        mm = product(bank[:, D * t:D * (t + 1)], lambda k: uT[:, t, k],
                                     lambda k: wqkv_sb[:, k, 2 * D:3 * D])
                    mm.then_inc(filled, 1)
                elif kind == "zb":
                    bank, filled = take("zb", n)
                    product(bank, lambda k: uT[:, 1, k], lambda k: wqkv_sb[:, k, 0:2 * D]).then_inc(filled, 1)
                elif kind == "qkT":
                    pe.wait_ge(parts_ready, n // CH + 1)
                    for parts, key in ((k_parts, "kT"), (q_parts, "qT")):
                        bank, filled = take(key, n)
                        for h in range(H // 2):
                            h0 = H * (n % CH) + 2 * h
                            mm = pe.transpose(bank.bitcast(F16)[:, P * h:P * (h + 1)],
                                              parts[:, h0:h0 + 2].rearrange("p h s e -> p (h s e)"), ident[:])
                        mm.then_inc(filled, 1)
                elif kind == "exp":
                    g, kt = ORDER[n // KTU]
                    b, qh, hg = group(g)
                    if n == 0:
                        for i in range(SCORES, SUMS):
                            pe.wait_ge(bank_free[i], BANK_USES[i])
                    for i, (sg, t0, _) in enumerate(STAGES):
                        if n % KTU == 0 and (g, kt) == (sg, t0):
                            pe.wait_ge(kz_sem(i), 32 * (g // 2 + 1) if g >= 2 else 32)
                    if n >= 2:
                        pe.wait_ge(probs_ready, n - 1)
                    for j in range(2):
                        mm = pe.matmul(sc_ps[:, n % 2, j], kz[:, g % 2, 2 * (n % 2) + j, P * kt:P * (kt + 1)],
                                       qT[:, b, 2 * hg + n % 2, QW * qh:QW * (qh + 1)], start=True, stop=True)
                    mm.then_inc(scores_ready, 1)
                elif kind == "sums":
                    g, kt = ORDER[n]
                    b, _, hg = group(g)
                    pe.wait_ge(probs_ready, KTU * (n + 1))
                    if n == 0:
                        pe.wait_ge(sums_zeroed, 1)
                    if kt == 0 and g >= 2:
                        pe.wait_ge(acc_ready, g - 1)
                    if g in (0, GROUPS // 2) and kt % CH == 0:
                        pe.wait_ge(values_ready, (TB * b + kt) // CH + 1)
                    for j in range(HG):
                        mm = pe.matmul(acc_ps[32 * j:32 * j + HD + 1, g % 2], v1[:, TB * b + kt, HG * hg + j],
                                       probs[:, n % RING, j], start=(kt == 0), stop=(kt == KT - 1),
                                       tile_position=(0, 32 * j))
                    mm.then_inc(sums_done, 1)
                elif kind == "accT":
                    bank, filled = take(kind, n)
                    pe.wait_ge(acc_ready, n + 1)
                    for t in range(UT):
                        mm = pe.transpose(bank[:, P * t:P * (t + 1)], accT[:, P * t:P * (t + 1)], identf[:])
                    mm.then_inc(filled, 1)
                elif kind == "oT":
                    drained(pe, "accT", (H // HG) * (n // 2 + 1) - 1)
                    bank, filled = take(kind, n)
                    turn(bank, [attn[2 * n // TB][:, (2 * n + t) % TB] for t in range(2)]).then_inc(filled, 1)
                elif kind == "y":
                    if n == 0:
                        pe.wait_ge(ld_o, 16)
                    drained(pe, "oT", n)
                    bank, filled = take(kind, n)
                    for t in range(2):
                        mm = product(bank[:, D * t:D * (t + 1)], lambda k: tTs[n // 2][:, 2 * (n % 2) + t, k],
                                     lambda k: wo_sb[:, k])
                    mm.then_inc(filled, 1)
                elif kind == "u2T":
                    pe.wait_ge(u2_ready, n // 2 + 1)
                    bank, filled = take(kind, n)
                    turn(bank, [u2[:, 2 * (n % 2) + t] for t in range(2)]).then_inc(filled, 1)
                elif kind in ("ffG", "ffF"):
                    if n == 0:
                        drained(pe, "foldB", 0)
                    drained(pe, "u2T", n)
                    bank, filled = take(kind, n)
                    part = slice(D, 2 * D) if kind == "ffG" else slice(0, D)
                    for t in range(2):
                        mm = product(bank[:, D * t:D * (t + 1)], lambda k: tTs[n // 2][:, 2 * (n % 2) + t, k],
                                     lambda k: fg[:, k, part])
                    mm.then_inc(filled, 1)

        @block.vector
        def _(dve):
            work = Work(dve, dve_chain)
            mark, after, link, tt, ts, stt = work.mark, work.after, work.link, work.tt, work.ts, work.stt
            def square(a, junk, total):
                return dve.tensor_tensor_reduce(junk, a, a, 1.0, 0.0, ALU.mult, ALU.add, total)

            def dots(a, b, o, uses):
                if uses > 1:
                    dve.wait_ge(dots_ready, uses - 1)
                done = []
                for t in range(UT):
                    if t >= 2:
                        after(done[t - 2])
                    ins = dve.tensor_tensor_reduce(dump[:, t % 2], a(t), b(t), 1.0, 0.0, ALU.mult, ALU.add,
                                                   o[:, t:t + 1])
                    if t < UT - 1:
                        done.append(mark(ins))
                ins.then_inc(dots_ready, 1)

            def atanh(o, n, w):
                om, c, e, num, den, sq_t = (t[:, 0:w] for t in rowt[4:10])
                link(ts(om, n, -1.25, ALU.mult, 1.25, ALU.add))
                link(ts(c.bitcast(I32), om.bitcast(I32), 0x7F800000, ALU.bitwise_and))
                link(stt(den, c, 1.0, n, ALU.subtract, ALU.mult))
                mark(stt(num, c, 1.0, n, ALU.add, ALU.mult))
                link(stt(den, c, 1.0, den, ALU.add, ALU.add))
                mark(stt(num, c, 1.0, num, ALU.subtract, ALU.add))
                link(dve.reciprocal(den, den))
                mark(ts(e.bitcast(I32), c.bitcast(I32), 23, ALU.logical_shift_right))
                link(tt(num, num, den, ALU.mult))
                mark(ts(e, e.bitcast(I32), 127.0, ALU.subtract, -math.log(2.0) / 2, ALU.mult))
                link(tt(sq_t, num, num, ALU.mult))
                link(ts(om, sq_t, ATANH[-1], ALU.mult))
                for coef in ATANH[-2:0:-1]:
                    link(stt(om, om, coef, sq_t, ALU.add, ALU.mult))
                link(stt(om, om, ATANH[0], num, ALU.add, ALU.mult))
                return tt(o, om, e, ALU.add)

            def row_norm(st, n2, w):
                t1, t2, n, s = (t[:, 0:w] for t in rowt[0:4])
                mean, var = st[:, :, 0], st[:, :, 1]
                link(tt(t1, mean, mean, ALU.mult))
                link(tt(t1, t1, var, ALU.add))
                mark(ts(n2, t1, float(D), ALU.mult))
                link(ts(t1, t1, float(D), ALU.mult, EPS2, ALU.max))
                work.rsqrt(t2, t1, n)
                link(tt(n, t1, t2, ALU.mult))
                link(ts(n, n, MAX_TANH, ALU.min))
                atanh(s, n, w).then_inc(logs_ready, 1)

            def row_stats(st, raw, done):
                for t, ready in enumerate(raw):
                    after(ready)
                    ins = dve.bn_aggr(st[:, t], bn[:, t])
                    if t < len(raw) - 1:
                        mark(ins)
                ins.then_inc(done, 1)

            def x_stats(b):
                raw = []
                for t in range(TB):
                    if t % 4 == 0:
                        dve.wait_ge(ld_x[2 * b + t // 4], 16)
                    raw.append(mark(dve.bn_stats(bn[:, t], x_sb[:, TB * b + t])))
                row_stats(stats[:, TB * b:TB * (b + 1)], raw, x_stats_ready)
                dve.wait_ge(x_stats_ready, b + 1)

            def modulate(o, rows, st, rstd, scale, shift, w, done):
                first = []
                for t in range(w + 1):
                    if t < w:
                        first.append(mark(stt(o(t), rows(t), st(t), scale, ALU.subtract, ALU.mult)))
                    if t:
                        after(first[t - 1])
                        stt(o(t - 1), o(t - 1), rstd(t - 1), shift, ALU.mult, ALU.add).then_inc(done, 1)

            def mobius_ab(uses):
                dve.wait_ge(ab_ready, uses)
                link(dve.reciprocal(t_, t_))
                tt(a_, a_, t_, ALU.mult).then_inc(a_ready, 1)
                link(tt(b_, b_, t_, ALU.mult))

            x_stats(0)
            row_norm(stats[:, 0:TB], x_n2[:, 0:TB], TB)
            dve.wait_ge(ld_bada, 16)
            for part in (SC1, SC2):
                mark(ts(bada_sb[:, D * part:D * (part + 1)], bada_sb[:, D * part:D * (part + 1)], 1.0, ALU.add))
            after(work.count)

            for kind, n in TIMELINE:
                if kind in TOKEN_STEPS and not on_pool(kind, n) and kind != "end_tanh":
                    token_step(work, kind, n)
                if kind == "ada_add":
                    bank, freed = full(dve, "ada", n)
                    tt(mods[:, n // 3, 2 * (n % 3):2 * (n % 3) + 2].rearrange("p m d -> p (m d)"), bank,
                       bada_sb[:, 512 * (n % 3):512 * (n % 3 + 1)], ALU.add).then_inc(freed, 1)
                elif kind == "x_stats":
                    x_stats(n)
                elif kind == "x_norm":
                    row_norm(stats[:, TB * n:TB * (n + 1)], x_n2[:, TB * n:TB * (n + 1)], TB)
                elif kind in ("u_first", "u_rest", "u"):
                    tiles = EARLY_TILES.get(kind, range(CH * n, CH * (n + 1)))
                    b = tiles.start // TB
                    if kind == "u_first":
                        drained(dve, "ada", 0)
                    if tiles.start in (0, TB):
                        dve.wait_ge(rstd_ready, b + 1)
                    modulate(lambda t: u_two[:, t] if kind == "u" else u_batch[:, tiles[t]],
                             lambda t: x_sb[:, tiles[t]], lambda t: stats[:, tiles[t], 0:1],
                             lambda t: x_rstd[:, tiles[t]:tiles[t] + 1], mods[:, b, SC1], mods[:, b, SH1],
                             len(tiles), u_ready)
                elif kind == "uT" and CH * n >= TB:
                    bank, freed = full(dve, kind, n)
                    dve.tensor_copy(uT.rearrange("p t k m -> p (t k m)"), bank).then_inc(freed, 1)
                elif kind in ("za", "zv", "zb"):
                    if n == 0:
                        dve.wait_ge(ld_bqkv, 16)
                    t0 = CH * n if CH * n < TB else 0
                    bank, freed = full(dve, kind, n)
                    if kind == "za":
                        if n:
                            dve.wait_ge(values_ready, n)
                        dve.wait_ge(ru_ready, 1 if n == 0 else max(2, n - TB // CH + 3))
                        stt(z[:, 0, 0:2 * D], bank, ru[:, t0:t0 + 1], bqkv_sb[:, 0:2 * D],
                            ALU.mult, ALU.add).then_inc(freed, 1)
                    elif kind == "zv":
                        mark(stt(z[:, 0, 2 * D:], bank[:, 0:D], ru[:, t0:t0 + 1], bqkv_sb[:, 2 * D:],
                                 ALU.mult, ALU.add))
                        stt(z[:, 1, 2 * D:], bank[:, D:2 * D], ru[:, t0 + 1:t0 + 2], bqkv_sb[:, 2 * D:],
                            ALU.mult, ALU.add).then_inc(freed, 1)
                    else:
                        stt(z[:, 1, 0:2 * D], bank, ru[:, t0 + 1:t0 + 2], bqkv_sb[:, 0:2 * D],
                            ALU.mult, ALU.add).then_inc(freed, 1)
                elif kind == "split":
                    if n:
                        dve.wait_ge(values_ready, n)
                    nh = CH * 3 * H
                    for t in range(CH):
                        dve.wait_ge(zsq_ready, CH * n + t + 1)
                        link(dve.tensor_reduce(ss[:, 3 * H * t:3 * H * (t + 1)],
                                               sqs[n][:, t].rearrange("p (h e) -> p h e", e=HD), AX_X, ALU.add))
                    link(dve.tensor_reduce(ss[:, nh:], ss[:, 0:nh].rearrange("p (s h) -> p s h", h=H), AX_X, ALU.add))
                    link(ts(ss, ss, EPS2, ALU.max))
                    work.rsqrt(rn, ss, split_t)
                    link(ts(rn[:, nh:], rn[:, nh:], C * A, ALU.mult, C, ALU.min))
                    stt(ss[:, 0:nh].rearrange("p (s h) -> p s h", h=H),
                        rn[:, 0:nh].rearrange("p (s h) -> p s h", h=H), A,
                        rn[:, nh:].unsqueeze(2).to_broadcast([P, CH * 3, H]), ALU.mult, ALU.min
                        ).then_inc(heads_ready, 1)
                elif kind == "parts":
                    dve.wait_ge(heads_ready, n + 1)
                    if n:
                        full(dve, "qT", CH * n - 1)
                    f = ss[:, 0:CH * 3 * H].rearrange("p (t h) -> p t h", t=CH)
                    qk = [mark(tt(z[:, t, 0:2 * D].rearrange("p (h e) -> p h e", e=HD),
                                  z[:, t, 0:2 * D].rearrange("p (h e) -> p h e", e=HD),
                                  f[:, t, 0:2 * H].unsqueeze(2).to_broadcast([P, 2 * H, HD]), ALU.mult))
                          for t in range(CH)]
                    his = []
                    for t in range(CH):
                        after(qk[t])
                        for s, parts in ((0, q_parts), (1, k_parts)):
                            his.append(mark(dve.tensor_copy(
                                parts[:, H * t:H * (t + 1), 0],
                                z[:, t, D * s:D * (s + 1)].rearrange("p (h e) -> p h e", e=HD))))
                    los = []
                    for t in range(CH):
                        for s, parts, lo in ((0, q_parts, 2), (1, k_parts, 1)):
                            after(his[2 * t + s])
                            los.append(mark(tt(parts[:, H * t:H * (t + 1), lo],
                                               z[:, t, D * s:D * (s + 1)].rearrange("p (h e) -> p h e", e=HD),
                                               parts[:, H * t:H * (t + 1), 0], ALU.subtract)))
                    mark(dve.tensor_copy(q_parts[:, :, 1], q_parts[:, :, 0]))
                    after(los[-1])
                    mark(dve.tensor_copy(q_parts[:, :, 3], q_parts[:, :, 2]))
                    dve.tensor_copy(k_parts[:, :, 2:4], k_parts[:, :, 0:2]).then_inc(parts_ready, 1)
                elif kind == "qkT" and n >= TB:
                    for key, dst in (("kT", kT), ("qT", qT)):
                        bank, freed = full(dve, key, n)
                        dve.tensor_copy(dst[:, 1, :, P * (n - TB):P * (n - TB + 1)],
                                        bank.bitcast(F16).rearrange("p (h m) -> p h m", m=P)).then_inc(freed, 1)
                elif kind == "sums_zero":
                    for i in range(SUMS, 8):
                        dve.wait_ge(bank_free[i], BANK_USES[i])
                    dve.memset(acc_ps[:], 0.0).then_inc(sums_zeroed, 1)
                elif kind == "accT":
                    b, qh, hg = group(n)
                    bank, freed = full(dve, kind, n)
                    rows = bank.rearrange("p (t h e) -> p t h e", h=HG, e=32)
                    if n:
                        drained(dve, "accT", n - 1)
                    link(dve.reciprocal(rden, rows[:, :, :, HD]))
                    o = attn[b][:, UT * qh:UT * (qh + 1), HG * HD * hg:HG * HD * (hg + 1)]
                    tt(o.rearrange("p t (h e) -> p t h e", e=HD), rows[:, :, :, 0:HD],
                       rden.unsqueeze(3).to_broadcast([P, UT, HG, HD]), ALU.mult).then_inc(freed, 1)
                elif kind in ("oT", "u2T"):
                    bank, freed = full(dve, kind, n)
                    dve.tensor_copy(tTs[n // 2][:, 2 * (n % 2):2 * (n % 2) + 2].rearrange("p t k m -> p (t k m)"), bank
                                    ).then_inc(freed, 1)
                elif kind == "y":
                    if n == 0:
                        dve.wait_ge(ld_bo, 16)
                    if n >= 2:
                        dve.wait_ge(out_ready, n // 2)
                    bank, freed = full(dve, kind, n)
                    mark(stt(y_sb[:, 2 * (n % 2)], bank[:, 0:D], 1.0 / C, bo_sb[:], ALU.mult, ALU.add))
                    stt(y_sb[:, 2 * (n % 2) + 1], bank[:, D:], 1.0 / C, bo_sb[:], ALU.mult, ALU.add).then_inc(freed, 1)
                elif kind == "gy":
                    drained(dve, "y", 2 * n + 1)
                    b = UT * n // TB
                    tt(x1, y_sb, mods[:, b, G1].unsqueeze(1).to_broadcast([P, UT, D]), ALU.mult).then_inc(gy_ready, 1)
                    dve.wait_ge(gy_ready, 2 * n + 1)
                    dots(lambda t: x1[:, t], lambda t: x_sb[:, UT * n + t], s3, 3 * n + 1)
                elif kind in ("mid_sq", "end_sq") and n < LAST_ROWS:
                    t, squares = n % UT, 2 * UT * (n // UT) + n % UT + (UT if kind == "end_sq" else 0)
                    if t == 0:
                        dve.wait_ge(dots_ready, 3 * (n // UT) + (3 if kind == "end_sq" else 1))
                    else:
                        dve.wait_ge(ysq_ready, squares)
                        after(first_square)
                    first_square = mark(square(y_sb[:, t], dump[:, 0], s1[:, t:t + 1]))
                    square((gz if kind == "end_sq" else x1)[:, t], dump[:, 1], s2[:, t:t + 1]).then_inc(ysq_ready, 1)
                elif kind == "u2_sq" and n < LAST_ROWS:
                    t = n % UT
                    dve.wait_ge(dots_ready, 3 * (n // UT) + 2)
                    if t >= 2:
                        dve.wait_ge(u2sq_ready, n - 1)
                    square(u2[:, t], dump[:, t % 2], usq2[:, t:t + 1]).then_inc(u2sq_ready, 1)
                elif kind == "x1":
                    mobius_ab(2 * n + 1)
                    if n < LAYER_UNITS - 1:
                        ax = [mark(ts(y_sb[:, t], x_sb[:, UT * n + t], a_[:, t:t + 1], ALU.mult)) for t in range(UT)]
                    sums, raw = [], []
                    for t in range(UT + 1):
                        if t < UT:
                            if n < LAYER_UNITS - 1:
                                after(ax[t])
                            else:
                                dve.wait_ge(ax_ready, t + 1)
                            sums.append(mark(stt(x1[:, t], x1[:, t], b_[:, t:t + 1], y_sb[:, t], ALU.mult, ALU.add)))
                        if t:
                            after(sums[t - 1])
                            raw.append(mark(dve.bn_stats(bn[:, t - 1], x1[:, t - 1])))
                    row_stats(st1, raw, stats_ready)
                elif kind == "x1_norm":
                    dve.wait_ge(stats_ready, n + 1)
                    row_norm(st1, n2_1, UT)
                elif kind == "u2":
                    b = UT * n // TB
                    dve.wait_ge(rstd_ready, B + n + 1)
                    for t in range(UT):
                        dve.wait_ge(centred_ready, UT * n + t + 1)
                        row = stt(u2[:, t], u2[:, t], rstd1[:, t:t + 1], mods[:, b, SH2], ALU.mult, ALU.add)
                        if t < UT - 1:
                            mark(row)
                        else:
                            row.then_inc(u2_ready, 1)
                    dve.wait_ge(u2_ready, n + 1)
                    dots(lambda t: u2[:, t], lambda t: fg_row[:, D:2 * D], d2, 3 * n + 2)
                elif kind == "ffG":
                    bank, freed = full(dve, kind, n)
                    for i in range(2):
                        t = 2 * (n % 2) + i
                        if i or n % 2:
                            after(first_ug)
                        else:
                            dve.wait_ge(dots_ready, 3 * (n // 2) + 2)
                            dve.wait_ge(u2sq_ready, UT * (n // 2 + 1))
                        ins = dve.tensor_tensor_reduce(dump[:, i], u2[:, t], bank[:, D * i:D * (i + 1)], 1.0, 0.0,
                                                       ALU.mult, ALU.add, d1[:, t:t + 1])
                        if i:
                            ins.then_inc(freed, 1)
                            drained(dve, kind, n)
                        else:
                            first_ug = mark(ins)
                elif kind == "ffF" and n // 2 < LAYER_UNITS - 1:
                    bank, freed = full(dve, kind, n)
                    dve.wait_ge(u2sq_ready, UT * (n // 2 + 1))
                    dve.tensor_copy(y_sb[:, 2 * (n % 2):2 * (n % 2) + 2], bank.rearrange("p (t d) -> p t d", t=2)
                                    ).then_inc(freed, 1)
                elif kind == "end_y":
                    b = UT * n // TB
                    dve.wait_ge(r1_ready, n + 1)
                    if n == 0:
                        dve.wait_ge(ld_b2, 16)
                    rows = []
                    for t in range(UT):
                        rows.append(mark(stt(gz[:, t], fg_row[:, 0:D], r1[:, t:t + 1], b2_sb[:], ALU.mult, ALU.add)))
                    for t in range(UT):
                        after(rows[t])
                        if n < LAYER_UNITS - 1:
                            product = y_sb[:, t]
                            drained(dve, "ffF", 2 * n + 1)
                        else:
                            bank, freed = full(dve, "ffF", 2 * n + t // 2)
                            product = bank[:, D * (t % 2):D * (t % 2 + 1)]
                        ins = stt(y_sb[:, t], product, r2[:, t:t + 1], gz[:, t], ALU.mult, ALU.add)
                        if n < LAYER_UNITS - 1:
                            rows[t] = mark(ins)
                        else:
                            ins.then_inc(y_ready, 1)
                    if n < LAYER_UNITS - 1:
                        after(rows[-1])
                    else:
                        dve.wait_ge(y_ready, UT)
                    tt(gz, y_sb, mods[:, b, G2].unsqueeze(1).to_broadcast([P, UT, D]), ALU.mult).then_inc(gy_ready, 1)
                    dve.wait_ge(gy_ready, 2 * n + 2)
                    dots(lambda t: gz[:, t], lambda t: x1[:, t], s3, 3 * n + 3)
                elif kind == "end_tanh":
                    if not on_pool(kind, n):
                        token_step(work, kind, n)
                    mobius_ab(2 * n + 2)
                    xa = [mark(stt(y_sb[:, t], x1[:, t], a_[:, t:t + 1], x_sb[:, UT * n + t], ALU.mult, ALU.add))
                          for t in range(UT)]
                    for t in range(UT):
                        after(xa[t])
                        last = stt(u2[:, t], gz[:, t], b_[:, t:t + 1], y_sb[:, t], ALU.mult, ALU.add)
                        if t < UT - 1:
                            mark(last)
                    last.then_inc(out_ready, 1)


class Work:

    def __init__(self, eng, chain, spare=None):
        self.eng, self.chain, self.spare, self.count = eng, chain, spare, 0

    def mark(self, ins):
        self.count += 1
        ins.then_inc(self.chain, 1)
        return self.count

    def after(self, n):
        self.eng.wait_ge(self.chain, n)

    def link(self, ins):
        self.after(self.mark(ins))

    def tt(self, o, a, b, op):
        return self.eng.tensor_tensor(o, a, b, op)

    def ts(self, o, a, s1, op1, s2=None, op2=None):
        if op2 is None:
            return self.eng.tensor_scalar(o, a, s1, None, op1)
        return self.eng.tensor_scalar(o, a, s1, s2, op1, op2)

    def stt(self, o, a, s, b, op1, op2):
        return self.eng.scalar_tensor_tensor(o, a, s, b, op1, op2)

    def mul(self, o, a, b):
        return self.tt(o, a, b, ALU.mult)

    def add(self, o, a, b):
        return self.tt(o, a, b, ALU.add)

    def rsqrt(self, y, a, t):
        link, ts, mul = self.link, self.ts, self.mul
        link(ts(y.bitcast(I32), a.bitcast(I32), -0.5, ALU.mult, float(0x5F1FFFF9), ALU.add))
        k0, k1 = 3 / 8 * 1.68191391, 3 / 8 * 0.703952253
        scale = 64 / 9
        link(mul(t, y, y))
        if self.spare is not None:
            u = self.spare[:, 0:t.shape[1]]
            link(mul(t, t, a))
            link(ts(t, t, -k1, ALU.mult, k0, ALU.add))
            link(mul(y, y, t))
            link(mul(t, y, y))
            link(mul(t, t, a))
            link(ts(u, t, scale * scale, ALU.mult, -scale * 10 / 3, ALU.add))
            link(mul(t, t, u))
            link(ts(t, t, 5.0, ALU.add))
            link(mul(y, y, t))
        else:
            link(self.stt(t, t, -k1, a, ALU.mult, ALU.mult))
            link(self.stt(y, t, k0, y, ALU.add, ALU.mult))
            link(mul(t, y, y))
            link(self.stt(t, t, scale, a, ALU.mult, ALU.mult))
            link(self.stt(t, t, -10 / 3, t, ALU.add, ALU.mult))
            link(self.stt(y, t, 5.0, y, ALU.add, ALU.mult))

    def clip(self, r, n2, t):
        self.link(self.ts(n2, n2, EPS2, ALU.max))
        self.rsqrt(r, n2, t)
        return self.ts(r, r, A, ALU.mult, 1.0, ALU.min)




def kernel(x, cond_1024, L0_cond_w_q, L0_cond_b_q, L0_cond_w_k, L0_cond_b_k, L0_cond_w_v, L0_cond_b_v,
           L0_cond_w_o, L0_cond_b_o, L0_cond_w_f1, L0_cond_b_f1, L0_cond_w_f2, L0_cond_b_f2,
           L0_cond_w_ada, L0_cond_b_ada):
    import concourse.bacc as bacc
    from concourse.bass_utils import run_bass_kernel_spmd

    def rows(w):
        w = np.asarray(w)
        return np.ascontiguousarray(w.reshape(-1, P, w.shape[-1]).transpose(1, 0, 2))

    w_qkv = np.concatenate([np.asarray(w) for w in (L0_cond_w_q, L0_cond_w_k, L0_cond_w_v)], axis=1)
    b_qkv = np.concatenate([np.asarray(b) for b in (L0_cond_b_q, L0_cond_b_k, L0_cond_b_v)])
    b1 = np.asarray(L0_cond_b_f1)
    arrays = {
        "in_x": rows(np.asarray(x).reshape(B * S, D)),
        "in_cond_t": rows(np.ascontiguousarray(np.asarray(cond_1024).T)),
        "in_w_ada": rows(L0_cond_w_ada), "in_b_ada": np.asarray(L0_cond_b_ada),
        "in_w_qkv": rows(w_qkv), "in_b_qkv": b_qkv,
        "in_w_o": rows(L0_cond_w_o), "in_b_o": np.asarray(L0_cond_b_o),
        "in_w_f1": rows(L0_cond_w_f1), "in_b_f1": b1,
        "in_b_f1_cols": np.ascontiguousarray(b1.reshape(KF, P).T),
        "in_w_f2": rows(L0_cond_w_f2), "in_b_f2": np.asarray(L0_cond_b_f2),
    }
    nc = bacc.Bacc("TRN2", target_bir_lowering=False, num_devices=1)
    ap = {k: nc.dram_tensor(k, a.shape, mybir.dt.from_np(a.dtype), kind="ExternalInput").ap()
          for k, a in arrays.items()}
    out = nc.dram_tensor("out_x", (P, TILES, D), F32, kind="ExternalOutput").ap()
    build(nc, ap["in_x"], ap["in_cond_t"], ap["in_w_ada"], ap["in_b_ada"], ap["in_w_qkv"], ap["in_b_qkv"],
          ap["in_w_o"], ap["in_b_o"], ap["in_w_f1"], ap["in_b_f1"], ap["in_b_f1_cols"], ap["in_w_f2"],
          ap["in_b_f2"], out)
    got = run_bass_kernel_spmd(nc, [arrays], core_ids=[0]).results[0]["out_x"]
    return got.transpose(1, 0, 2).reshape(B, S, D)
```
